# Optimizing a Trainium2 kernel written in Bass

```python
import numpy as np
import jax
import jax.numpy as jnp

def _softmax(x, axis=-1):
    return jax.nn.softmax(x, axis=axis)

def _gelu(x):
    return jax.nn.gelu(x, approximate=True)

def _silu(x):
    return jax.nn.silu(x)

def _sigmoid(x):
    return jax.nn.sigmoid(x)

def _layernorm(x, axis=-1, eps=1e-05):
    m = jnp.mean(x, axis=axis, keepdims=True)
    v = jnp.var(x, axis=axis, keepdims=True)
    return (x - m) / jnp.sqrt(v + eps)

def _scatter_add(tgt, idx, src, axis=0):
    return tgt.at[idx].add(src)

def _segment_sum(src, seg, n):
    return jax.ops.segment_sum(src, seg, n)
kernel_name = 'mk_xattn_ffn_d1_seqx_r8_07fe79'

def setup_inputs(seed: int=0):
    np.random.seed(seed)
    _w = jnp.asarray

    def _rec_inputs():
        import jax
        import jax.numpy as jnp
        _rk = jax.random.key(seed)
        x = -0.0003929 + 0.9999 * jax.random.normal(jax.random.fold_in(_rk, 1), (32, 64, 512), jnp.float32)
        _lenS = 64 - jax.random.randint(jax.random.fold_in(_rk, 7), (32,), 0, max(1, 64 // 4) + 1, jnp.int32)
        _lenS2 = 64 - jax.random.randint(jax.random.fold_in(_rk, 8), (32,), 0, max(1, 64 // 4) + 1, jnp.int32)
        _ctx_4096P = jax.random.normal(jax.random.fold_in(_rk, 11), (32, 16, 512), jnp.float32)
        _ctx_4096c = jax.random.dirichlet(jax.random.fold_in(_rk, 511), 0.3 * jnp.ones((16,), jnp.float32), (32, 64))
        _ctx_4096t = jnp.einsum('bsk,bkd->bsd', _ctx_4096c, _ctx_4096P)
        _ctx_4096t = _ctx_4096t * jax.lax.rsqrt(jnp.mean(jnp.square(_ctx_4096t)) + 1e-12) * 0.953939
        ctx_4096 = 2.81802e-05 + 1.00001 * (_ctx_4096t + 0.3 * jax.random.normal(jax.random.fold_in(_rk, 611), (32, 64, 512), jnp.float32))
        return (x, ctx_4096)
    x, ctx_4096 = _rec_inputs()

    def _L0_xattn_setup():
        import jax, jax.numpy as jnp
        import numpy as np
        DIM = 64
        HEADS = 8
        DIM_HEAD = 64
        HIDDEN = HEADS * DIM_HEAD
        SCALE = DIM_HEAD ** (-0.5)
        key = jax.random.key(seed)
        ks = jax.random.split(key, 9)
        b, n = (8, 512)
        std = 1.0 / np.sqrt(DIM)
        return {'q': jax.random.normal(ks[0], (b, DIM, n), jnp.float32), 'k': jax.random.normal(ks[1], (b, DIM, n), jnp.float32), 'v': jax.random.normal(ks[2], (b, DIM, n), jnp.float32), 'Wq': jax.random.normal(ks[3], (HIDDEN, DIM), jnp.float32) * std, 'Wk': jax.random.normal(ks[4], (HIDDEN, DIM), jnp.float32) * std, 'Wv': jax.random.normal(ks[5], (HIDDEN, DIM), jnp.float32) * std, 'Wo': jax.random.normal(ks[6], (DIM, HIDDEN), jnp.float32) * (1.0 / np.sqrt(HIDDEN)), 'bo': jax.random.normal(ks[7], (DIM,), jnp.float32) * 0.01, 'g': jnp.ones((1, DIM, 1), jnp.float32)}
    _L0_xattn_all = _L0_xattn_setup()
    _L0_xattn_in = {k: v for k, v in _L0_xattn_all.items() if k in ('Wq', 'Wk', 'Wv', 'Wo', 'bo', 'g')}
    del _L0_xattn_all

    def _L0_ffn_setup():
        import jax, jax.numpy as jnp
        import numpy as np
        DIM = 512
        INTER = 1792
        SPARSITY = 32
        RANK = 16
        key = jax.random.key(seed)
        ks = jax.random.split(key, 5)
        B, T = (32, 1)
        x = jax.random.normal(ks[0], (B, T, DIM), dtype=jnp.float32)
        c1_w = jax.random.normal(ks[1], (RANK, DIM), dtype=jnp.float32) * (1.0 / np.sqrt(DIM))
        c2_w = jax.random.normal(ks[2], (INTER, RANK), dtype=jnp.float32) * (1.0 / np.sqrt(RANK))
        w1 = jax.random.normal(ks[3], (INTER, DIM), dtype=jnp.float32) * (1.0 / np.sqrt(DIM))
        w2t = jax.random.normal(ks[4], (INTER, DIM), dtype=jnp.float32) * (1.0 / np.sqrt(INTER))
        return {'x': x, 'c1_w': c1_w, 'c2_w': c2_w, 'w1': w1, 'w2t': w2t}
    _L0_ffn_all = _L0_ffn_setup()
    _L0_ffn_in = {k: v for k, v in _L0_ffn_all.items() if k in ('c1_w', 'c2_w', 'w1', 'w2t')}
    del _L0_ffn_all
    return {'x': x, 'ctx_4096': ctx_4096, 'L0_xattn_Wq': _L0_xattn_in['Wq'], 'L0_xattn_Wk': _L0_xattn_in['Wk'], 'L0_xattn_Wv': _L0_xattn_in['Wv'], 'L0_xattn_Wo': _L0_xattn_in['Wo'], 'L0_xattn_bo': _L0_xattn_in['bo'], 'L0_xattn_g': _L0_xattn_in['g'], 'L0_ffn_c1_w': _L0_ffn_in['c1_w'], 'L0_ffn_c2_w': _L0_ffn_in['c2_w'], 'L0_ffn_w1': _L0_ffn_in['w1'], 'L0_ffn_w2t': _L0_ffn_in['w2t']}

def reference(x, ctx_4096, L0_xattn_Wq, L0_xattn_Wk, L0_xattn_Wv, L0_xattn_Wo, L0_xattn_bo, L0_xattn_g, L0_ffn_c1_w, L0_ffn_c2_w, L0_ffn_w1, L0_ffn_w2t):
    import jax
    import jax.numpy as jnp

    def _L0_xattn_ref(q, k, v, Wq, Wk, Wv, Wo, bo, g):
        import jax, jax.numpy as jnp
        import numpy as np
        DIM = 64
        HEADS = 8
        DIM_HEAD = 64
        HIDDEN = HEADS * DIM_HEAD
        SCALE = DIM_HEAD ** (-0.5)
        b = q.shape[0]
        qh = jnp.einsum('bcn,oc->bon', q, Wq).reshape(b, HEADS, DIM_HEAD, -1)
        kh = jnp.einsum('bcn,oc->bon', k, Wk).reshape(b, HEADS, DIM_HEAD, -1)
        vh = jnp.einsum('bcn,oc->bon', v, Wv).reshape(b, HEADS, DIM_HEAD, -1)
        qh = jax.nn.softmax(qh, axis=-2) * SCALE
        kh = jax.nn.softmax(kh, axis=-1)
        context = jnp.einsum('bhdn,bhen->bhde', kh, vh)
        out = jnp.einsum('bhde,bhdn->bhen', context, qh)
        out = out.reshape(b, HIDDEN, -1)
        out = jnp.einsum('bcn,oc->bon', out, Wo) + bo[None, :, None]
        norm = jnp.maximum(jnp.sqrt(jnp.sum(out * out, axis=1, keepdims=True)), 1e-12)
        return out / norm * g * np.sqrt(DIM)

    def _L0_ffn_ref(x, c1_w, c2_w, w1, w2t):
        import jax, jax.numpy as jnp
        import numpy as np
        DIM = 512
        INTER = 1792
        SPARSITY = 32
        RANK = 16
        B, T, M = x.shape
        xf = x.reshape(B * T, M)
        inter = xf @ c1_w.T @ c2_w.T
        n_blocks = INTER // SPARSITY
        blk = inter.reshape(B * T, n_blocks, SPARSITY)
        idx = jnp.argmax(blk, axis=-1) + jnp.arange(0, INTER, SPARSITY)
        w1_g = w1[idx]
        w2_g = w2t[idx]
        h = jax.nn.relu(jnp.einsum('bkm,bm->bk', w1_g, xf))
        out = jnp.einsum('bk,bkm->bm', h, w2_g)
        return out.reshape(B, T, M)
    x = x + _L0_xattn_ref(_layernorm(x, axis=-1), ctx_4096, ctx_4096, L0_xattn_Wq, L0_xattn_Wk, L0_xattn_Wv, L0_xattn_Wo, L0_xattn_bo, L0_xattn_g)
    x = x + _L0_ffn_ref(_layernorm(x, axis=-1), L0_ffn_c1_w, L0_ffn_c2_w, L0_ffn_w1, L0_ffn_w2t)
    return x

_drawn_inputs = setup_inputs


def setup_inputs(seed=0):
    import zlib

    import numpy as np

    out = dict(_drawn_inputs(seed))
    spreads = {'L0_xattn_g': (1.0, 0.2)}
    factors = {}
    for name, (base, spread) in spreads.items():
        noise = np.random.default_rng([zlib.crc32(name.encode()), seed]).standard_normal(out[name].shape)
        drawn = base * np.exp(spread * noise) if base else spread * noise
        out[name] = jnp.asarray(drawn.astype(out[name].dtype))
    for name, factor in factors.items():
        out[name] = (out[name] * factor).astype(out[name].dtype)
    return out
```

```python
from contextlib import ExitStack

import concourse.bass as bass
from concourse import mybir

fp32 = mybir.dt.float32
f32r = mybir.dt.float32r
bf16 = mybir.dt.bfloat16
ALU = mybir.AluOpType
ACT = mybir.ActivationFunctionType
AX = mybir.AxisListType

B, C, N = 32, 64, 512
HEADS, D = 8, 64
HID = HEADS * D
P = 128
NT = N // P
HT = HID // P
SCALE = float(D) ** -0.5
EPS = 1e-5
NORM_EPS = 1e-12
INTER, SPARSE, RANK = 1792, 32, 16
MT = N // P
KT = INTER // P
FFN_COLS = MT * INTER + KT * N
SPLIT = FFN_COLS // B
TILES = B * C // P
CHUNK = 512
CHUNKS = [(off, min(CHUNK, INTER - off)) for off in range(0, INTER, CHUNK)]
NC = len(CHUNKS)
FIRST_LOOPED, LAST_LOOPED = 5, B - 4


def later(value):
    return not isinstance(value, int) or value > 0


def steps(eng, step):
    for g in range(-1, FIRST_LOOPED):
        step(g, g // 2, g % 2, g)
    with eng.Fori(FIRST_LOOPED // 2, LAST_LOOPED // 2) as k:
        step(2 * k + 1, k, 1, None)
        step(2 * k + 2, k + 1, 0, None)
    for g in range(LAST_LOOPED + 1, B + 2):
        step(g, g // 2, g % 2, g)


def real(known, shift):
    return known is None or 0 <= known + shift < B


def attention_phase(nc, A, weights_hi, weights_lo, scratch):
    with ExitStack() as ctx:
        sb = lambda name, shape, dt=fp32: ctx.enter_context(nc.sbuf_tensor(name, shape, dt))
        ps = lambda name, shape: ctx.enter_context(nc.psum_tensor(name, shape, fp32))
        sem = lambda name: ctx.enter_context(nc.semaphore(name))

        w_raw = sb("w_raw", [P, 2, HID])
        wq_hi, wq_lo = sb("wq_hi", [P, HID], f32r), sb("wq_lo", [P, HID], f32r)
        wk_hi, wk_lo = sb("wk_hi", [P, HID], f32r), sb("wk_lo", [P, HID], f32r)
        wv, woT = sb("wv", [D, HEADS, C]), sb("woT", [D, HEADS, C])
        vo = sb("vo", [C, HEADS, C])
        bo = sb("bo", [P, 1])
        ident = sb("ident", [P, P])
        stage = [sb(f"stage{i}", [P, SPLIT]) for i in range(2)]
        x_in = [sb(f"x_in{i}", [P, N]) for i in range(2)]
        c_in = [sb(f"c_in{i}", [P, N]) for i in range(2)]
        ctxT = [sb(f"ctxT{i}", [P, NT, C]) for i in range(2)]
        x_split = [sb(f"x_split{i}", [P, N], f32r) for i in range(2)]
        c_split = [sb(f"c_split{i}", [P, N], f32r) for i in range(2)]
        xn = sb("xn", [P, N])
        stats = sb("stats", [P, 6])
        moments = [sb(f"moments{i}", [P, 2]) for i in range(2)]
        var_eps = sb("var_eps", [P, 1])
        neg_half, eps = sb("neg_half", [P, 1]), sb("eps", [P, 1])
        rstd = [sb(f"rstd{i}", [P, 1]) for i in range(2)]
        E = [sb(f"E{i}", [P, HT, N]) for i in range(2)]
        neg_kmax = [sb(f"neg_kmax{i}", [P, HT]) for i in range(2)]
        ksum = [sb(f"ksum{i}", [P, HT]) for i in range(2)]
        krec = sb("krec", [P, HT])
        Q = [sb(f"Q{i}", [P, NT, HID]) for i in range(2)]
        HALF = NT * HEADS // 2
        qmax = sb("qmax", [P, 2, HALF])
        qsum = sb("qsum", [P, 2, HALF])
        qrec = [sb(f"qrec{i}", [P, 2, HALF]) for i in range(2)]
        ET = [sb(f"ET{i}", [P, HID]) for i in range(2)]
        QT = [sb(f"QT{i}", [P, N]) for i in range(2)]
        PT = sb("PT", [C, HID])
        G = [sb(f"G{i}", [P, HT, C]) for i in range(2)]
        out_sb = [sb(f"out_sb{i}", [P, N]) for i in range(2)]

        slot = [ps(f"slot{i}", [P, 2, 512]) for i in range(2)]
        turn_e, turn_q = ps("turn_e", [P, 512]), ps("turn_q", [P, 512])
        pg = ps("pg", [P, 512])
        acc = ps("acc", [P, 512])

        consts_in = sem("consts_in")
        w_hi, w_lo, vo_mm, vo_ready = sem("w_hi"), sem("w_lo"), sem("vo_mm"), sem("vo_ready")
        x_loaded = [sem(f"x_loaded{i}") for i in range(2)]
        c_loaded = [sem(f"c_loaded{i}") for i in range(2)]
        ctxT_loaded = [sem(f"ctxT_loaded{i}") for i in range(2)]
        stage_loaded = [sem(f"stage_loaded{i}") for i in range(2)]
        stage_hi, stage_done = sem("stage_hi"), sem("stage_done")
        x_moments, x_var, x_rstd = sem("x_moments"), sem("x_var"), sem("x_rstd")
        x_normed, x_hi, x_ready = sem("x_normed"), sem("x_hi"), sem("x_ready")
        c_hi, c_ready = sem("c_hi"), sem("c_ready")
        k_proj, k_max, k_exped, k_rec = sem("k_proj"), sem("k_max"), sem("k_exped"), sem("k_rec")
        q_proj, q_max, q_shifted, q_exped = sem("q_proj"), sem("q_max"), sem("q_shifted"), sem("q_exped")
        q_sum, q_rec, q_scaled = sem("q_sum"), sem("q_rec"), sem("q_scaled")
        e_turned, e_copied, p_mm, p_copied = sem("e_turned"), sem("e_copied"), sem("p_mm"), sem("p_copied")
        q_turned, q_copied, out_mm, out_copied = sem("q_turned"), sem("q_copied"), sem("out_mm"), sem("out_copied")
        g_mm, g_ready = sem("g_mm"), sem("g_ready")
        stored = [sem(f"stored{i}") for i in range(2)]
        powers_set = sem("powers_set")

        heads = lambda ap: ap.rearrange("p a (h d) -> p (a h) d", d=D)
        CONSTS = 5

        with nc.Block() as block:

            @block.sync
            def _(sp):
                def load_x(g, k, par):
                    for r in (0, C):
                        sp.dma_start(x_in[par][r:r + C, :], A["x"][g]).then_inc(x_loaded[par], 16)

                def load_c(g, k, par):
                    for r in (0, C):
                        sp.dma_start(c_in[par][r:r + C, :], A["ctx"][g]).then_inc(c_loaded[par], 16)

                def load_ctxT(g, par):
                    sp.dma_start(ctxT[par][:], A["ctxT"][g]).then_inc(ctxT_loaded[par], 16)

                def load_stage(g, par):
                    sp.dma_start(stage[par][:], A["ffn_w"][g]).then_inc(stage_loaded[par], 16)

                load_x(0, 0, 0)
                sp.dma_start(w_raw[:], A["wqk"]).then_inc(consts_in, 16)
                load_c(0, 0, 0)
                sp.dma_start(wv[:], A["wv"]).then_inc(consts_in, 16)
                sp.dma_start(woT[:], A["woT"]).then_inc(consts_in, 16)
                sp.dma_start(bo[C:P, :], A["bo"]).then_inc(consts_in, 16)
                sp.dma_start(ident[:], A["ident"]).then_inc(consts_in, 16)
                load_x(1, 0, 1)
                load_c(1, 0, 1)
                load_ctxT(0, 0)
                load_stage(0, 0)
                load_stage(1, 1)

                def step(g, k, par, known):
                    if known == -1:
                        return
                    if real(known, 2):
                        sp.wait_ge(x_ready, g + 1)
                        load_x(g + 2, k + 1, par)
                        sp.wait_ge(c_ready, g + 1)
                        load_c(g + 2, k + 1, par)
                        sp.wait_ge(stage_done, g + 1)
                        load_stage(g + 2, par)
                    if real(known, 1):
                        if later(NT * g):
                            sp.wait_ge(p_mm, NT * g)
                        load_ctxT(g + 1, 1 - par)
                    if real(known, -2):
                        sp.wait_ge(out_copied, g - 1)
                        sp.dma_start(scratch[g - 2], out_sb[par][C:P, :]).then_inc(stored[par], 16)

                steps(sp, step)
                for s in stored:
                    sp.wait_ge(s, 16 * (B // 2))

            @block.gpsimd
            def _(pool):
                nc.gpsimd.memset(neg_half[:], -0.5).then_inc(powers_set, 1)
                nc.gpsimd.memset(eps[:], EPS).then_inc(powers_set, 1)
                pool.wait_ge(powers_set, 2)

                def step(g, k, par, known):
                    if later(g + 1 if known is None else min(g + 1, B)):
                        pool.wait_ge(c_ready, g + 1 if known is None else min(g + 1, B))
                    if real(known, 1):
                        pool.wait_ge(x_moments, g + 2)
                        nc.gpsimd.tensor_tensor(var_eps[:], moments[1 - par][:, 1:2], eps[:],
                                                ALU.add).then_inc(x_var, 1)
                        pool.wait_ge(x_var, g + 2)
                        nc.gpsimd.tensor_tensor(rstd[1 - par][:], var_eps[:], neg_half[:],
                                                ALU.pow).then_inc(x_rstd, 1)
                    if real(known, 0):
                        cols = bass.ds(g * SPLIT, SPLIT)
                        pool.wait_ge(stage_loaded[par], 16 * (k + 1))
                        nc.gpsimd.tensor_copy(weights_hi[:, cols], stage[par][:]).then_inc(stage_hi, 1)
                        pool.wait_ge(stage_hi, g + 1)
                        nc.gpsimd.tensor_tensor(weights_lo[:, cols], stage[par][:],
                                                weights_hi[:, cols].bitcast(fp32),
                                                ALU.subtract).then_inc(stage_done, 1)
                    if real(known, -1):
                        for s in range(2):
                            pool.wait_ge(q_rec, 2 * g - 1 + s)
                            half = heads(Q[1 - par][:, 2 * s:2 * s + 2, :])
                            nc.gpsimd.tensor_tensor(
                                half, half, qrec[1 - par][:, s, :].unsqueeze(2).broadcast_to([P, HALF, D]),
                                ALU.mult).then_inc(q_scaled, 1)
                    if real(known, 1):
                        pool.wait_ge(x_rstd, g + 2)
                        if later(g + 1):
                            pool.wait_ge(stage_done, g + 1)
                        if later(2 * g):
                            pool.wait_ge(q_scaled, 2 * g)
                        pool.wait_ge(x_hi, g + 2)
                        nc.gpsimd.tensor_tensor(x_split[1 - par][C:P, :], xn[C:P, :],
                                                x_split[1 - par][C:P, :].bitcast(fp32),
                                                ALU.subtract).then_inc(x_ready, 1)
                        pool.wait_ge(c_hi, g + 2)
                        nc.gpsimd.tensor_tensor(c_split[1 - par][C:P, :], c_in[1 - par][C:P, :],
                                                c_split[1 - par][C:P, :].bitcast(fp32),
                                                ALU.subtract).then_inc(c_ready, 1)

                steps(pool, step)

            @block.vector
            def _(dve):
                def prologue():
                    dve.wait_ge(consts_in, 16 * CONSTS)
                    for n, (hi, lo) in enumerate(((wq_hi, wq_lo), (wk_hi, wk_lo))):
                        nc.vector.tensor_copy(hi[:], w_raw[:, n, :]).then_inc(w_hi, 1)
                        dve.wait_ge(w_hi, n + 1)
                        nc.vector.tensor_tensor(lo[:], w_raw[:, n, :], hi[:].bitcast(fp32),
                                                ALU.subtract).then_inc(w_lo, 1)
                    dve.wait_ge(vo_mm, 1)
                    nc.vector.tensor_copy(vo[:], acc[0:C, :].rearrange("c (h o) -> c h o", h=HEADS))\
                        .then_inc(vo_ready, 1)

                def step(g, k, par, known):
                    if real(known, -1):
                        for s in range(2):
                            dve.wait_ge(q_proj, 2 * g - 1 + s)
                            src = heads(slot[s][:])
                            nc.vector.tensor_reduce(qmax[:, s, :], src, AX.X, ALU.max).then_inc(q_max, 1)
                            dve.wait_ge(q_max, 2 * g - 1 + s)
                            if later(HT * (g - 2)):
                                dve.wait_ge(q_turned, HT * (g - 2))
                            nc.vector.tensor_tensor(
                                heads(Q[1 - par][:, 2 * s:2 * s + 2, :]), src,
                                qmax[:, s, :].unsqueeze(2).broadcast_to([P, HALF, D]),
                                ALU.subtract).then_inc(q_shifted, 1)
                    if real(known, 1):
                        dve.wait_ge(x_loaded[1 - par], 32 * ((k if par == 0 else k + 1) + 1))
                        nc.vector.bn_stats(stats[:], x_in[1 - par][:])
                        dve.drain()
                        nc.vector.bn_aggr(moments[1 - par][:], stats[:]).then_inc(x_moments, 1)
                    if known == -1:
                        prologue()
                    if real(known, 0):
                        for s in range(2):
                            dve.wait_ge(k_proj, 2 * g + s + 1)
                            nc.vector.tensor_reduce(neg_kmax[par][:, 2 * s:2 * s + 2], slot[s][:], AX.X, ALU.max,
                                                    negate=True).then_inc(k_max, 1)
                    if real(known, -1):
                        for s in range(2):
                            dve.wait_ge(q_exped, 2 * g - 1 + s)
                            nc.vector.tensor_reduce(qsum[:, s, :], heads(Q[1 - par][:, 2 * s:2 * s + 2, :]),
                                                    AX.X, ALU.add).then_inc(q_sum, 1)
                            dve.wait_ge(q_sum, 2 * g - 1 + s)
                            if later(2 * g - 4):
                                dve.wait_ge(q_scaled, 2 * g - 4)
                            nc.vector.reciprocal(qrec[1 - par][:, s, :], qsum[:, s, :]).then_inc(q_rec, 1)
                    if real(known, 1):
                        dve.wait_ge(x_rstd, g + 2)
                        if later(g + 1):
                            dve.wait_ge(x_ready, g + 1)
                        nc.vector.tensor_scalar(xn[:], x_in[1 - par][:], moments[1 - par][:, 0:1],
                                                rstd[1 - par][:], ALU.subtract, ALU.mult).then_inc(x_normed, 1)
                        dve.wait_ge(x_normed, g + 2)
                        if later(2 * g):
                            dve.wait_ge(q_proj, 2 * g)
                        nc.vector.tensor_copy(x_split[1 - par][:], xn[:]).then_inc(x_hi, 1)
                        dve.wait_ge(c_loaded[1 - par], 32 * ((k if par == 0 else k + 1) + 1))
                        if later(2 * g):
                            dve.wait_ge(k_proj, 2 * g)
                        nc.vector.tensor_copy(c_split[1 - par][:], c_in[1 - par][:]).then_inc(c_hi, 1)
                    if real(known, -1):
                        dve.wait_ge(k_exped, 2 * g)
                        nc.vector.reciprocal(krec[:], ksum[1 - par][:]).then_inc(k_rec, 1)
                        dve.wait_ge(k_rec, g)
                        dve.wait_ge(g_mm, g)
                        nc.vector.scalar_tensor_tensor(
                            G[1 - par][:], pg[:, 0:HT * C].rearrange("p (j o) -> p j o", j=HT), SCALE,
                            krec[:].unsqueeze(2).broadcast_to([P, HT, C]), ALU.mult, ALU.mult)\
                            .then_inc(g_ready, 1)

                steps(dve, step)

            @block.scalar
            def _(act):
                def step(g, k, par, known):
                    def exp_q(s):
                        if real(known, -1):
                            act.wait_ge(q_shifted, 2 * g - 1 + s)
                            half = Q[1 - par][:, 2 * s:2 * s + 2, :]
                            nc.scalar.activation(half, half, ACT.Exp).then_inc(q_exped, 1)

                    def exp_k(s):
                        if real(known, 0):
                            act.wait_ge(k_max, 2 * g + s + 1)
                            if later(NT * (g - 1)):
                                act.wait_ge(e_turned, NT * (g - 1))
                            if later(g - 1):
                                act.wait_ge(k_rec, g - 1)
                            for i in range(2):
                                j = 2 * s + i
                                last = nc.scalar.activation(E[par][:, j, :], slot[s][:, i, :], ACT.Exp,
                                                            bias=neg_kmax[par][:, j:j + 1],
                                                            accum_out=ksum[par][:, j:j + 1])
                            last.then_inc(k_exped, 1)

                    def copy(m):
                        if real(known, -1):
                            use = NT * (g - 1) + m
                            act.wait_ge(e_turned, use + 1)
                            if later(use - 1):
                                act.wait_ge(p_mm, use - 1)
                            nc.scalar.activation(ET[m % 2][:], turn_e[:], ACT.Copy).then_inc(e_copied, 1)
                        if real(known, -2):
                            use = HT * (g - 2) + m
                            act.wait_ge(q_turned, use + 1)
                            if later(use - 1):
                                act.wait_ge(out_mm, use - 1)
                            nc.scalar.activation(QT[m % 2][:], turn_q[:], ACT.Copy).then_inc(q_copied, 1)

                    exp_q(0)
                    copy(0)
                    exp_q(1)
                    copy(1)
                    exp_k(0)
                    copy(2)
                    exp_k(1)
                    copy(3)
                    if real(known, -1):
                        act.wait_ge(p_mm, NT * g)
                        nc.scalar.activation(PT[:], pg[0:C, :], ACT.Copy).then_inc(p_copied, 1)
                    if real(known, -2):
                        act.wait_ge(out_mm, HT * (g - 1))
                        if later(16 * (k - 1)):
                            act.wait_ge(stored[par], 16 * (k - 1))
                        nc.scalar.activation(out_sb[par][C:P, :], acc[C:P, :], ACT.Identity,
                                             bias=bo[C:P, :]).then_inc(out_copied, 1)

                act.wait_ge(consts_in, 16 * CONSTS)
                steps(act, step)

            @block.tensor
            def _(pe):
                pe.wait_ge(consts_in, 16 * CONSTS)
                for h in range(HEADS):
                    last = nc.tensor.matmul(acc[0:C, h * C:(h + 1) * C], wv[:, h, :], woT[:, h, :],
                                            start=True, stop=True)
                last.then_inc(vo_mm, 1)

                def step(g, k, par, known):
                    if known == -1:
                        return

                    def turn(m):
                        if real(known, -1):
                            if later(NT * (g - 1) + m):
                                pe.wait_ge(e_copied, NT * (g - 1) + m)
                            pe.wait_ge(k_exped, 2 * g)
                            for j in range(HT):
                                last = nc.tensor.transpose(turn_e[:, j * P:(j + 1) * P],
                                                           E[1 - par][:, j, m * P:(m + 1) * P], ident[:])
                            last.then_inc(e_turned, 1)
                        if real(known, -2):
                            if later(HT * (g - 2) + m):
                                pe.wait_ge(q_copied, HT * (g - 2) + m)
                            pe.wait_ge(q_scaled, 2 * g - 2)
                            for t in range(NT):
                                last = nc.tensor.transpose(turn_q[:, t * P:(t + 1) * P],
                                                           Q[par][:, t, m * P:(m + 1) * P], ident[:])
                            last.then_inc(q_turned, 1)

                    def products(m):
                        if real(known, -1):
                            pe.wait_ge(e_copied, NT * (g - 1) + m + 1)
                            if m == 0:
                                pe.wait_ge(ctxT_loaded[1 - par], 16 * ((k - 1 if par == 0 else k) + 1))
                                if later(g - 1):
                                    pe.wait_ge(g_ready, g - 1)
                        if real(known, -2):
                            pe.wait_ge(q_copied, HT * (g - 2) + m + 1)
                            if m == 0:
                                pe.wait_ge(g_ready, g - 1)
                                if later(g - 2):
                                    pe.wait_ge(out_copied, g - 2)
                        if real(known, -1):
                            nc.tensor.matmul(pg[0:C, :], ctxT[1 - par][:, m, :], ET[m % 2][:],
                                             start=(m == 0), stop=(m == NT - 1)).then_inc(p_mm, 1)
                        if real(known, -2):
                            nc.tensor.matmul(acc[C:P, :], G[par][:, m, :], QT[m % 2][:],
                                             start=(m == 0), stop=(m == HT - 1)).then_inc(out_mm, 1)

                    turn(0)
                    turn(1)
                    products(0)
                    if real(known, 0):
                        pe.wait_ge(c_ready, g + 1)
                        pe.wait_ge(w_lo, 2)
                        for s in range(2):
                            if later(2 * g - 1 + s):
                                pe.wait_ge(q_shifted, 2 * g - 1 + s)
                            for i in range(2):
                                j = slice((2 * s + i) * P, (2 * s + i + 1) * P)
                                nc.tensor.matmul(slot[s][:, i, :], wk_hi[:, j], c_split[par][:], start=True, stop=False)
                                last = nc.tensor.matmul(slot[s][:, i, :], wk_lo[:, j], c_split[par][:], start=False, stop=True)
                            last.then_inc(k_proj, 1)
                    turn(2)
                    products(1)
                    turn(3)
                    products(2)
                    products(3)
                    if real(known, 0):
                        pe.wait_ge(x_ready, g + 1)
                        for s in range(2):
                            pe.wait_ge(k_exped, 2 * g + s + 1)
                            for i in range(2):
                                t = slice((2 * s + i) * P, (2 * s + i + 1) * P)
                                nc.tensor.matmul(slot[s][:, i, :], x_split[par][:, t], wq_hi[:], start=True, stop=False)
                                last = nc.tensor.matmul(slot[s][:, i, :], x_split[par][:, t], wq_lo[:], start=False, stop=True)
                            last.then_inc(q_proj, 1)
                    if real(known, -1):
                        pe.wait_ge(vo_ready, 1)
                        pe.wait_ge(p_copied, g)
                        for h in range(HEADS):
                            r = (h % 2) * D
                            last = nc.tensor.matmul(pg[r:r + D, (h // 2) * C:(h // 2 + 1) * C],
                                                    PT[:, h * D:(h + 1) * D], vo[:, h, :], start=True, stop=True)
                        last.then_inc(g_mm, 1)

                steps(pe, step)


def ffn_phase(nc, A, weights_hi, weights_lo, scratch, out):
    with ExitStack() as ctx:
        sb = lambda name, shape, dt=fp32: ctx.enter_context(nc.sbuf_tensor(name, shape, dt))
        ps = lambda name, shape: ctx.enter_context(nc.psum_tensor(name, shape, fp32))
        sem = lambda name: ctx.enter_context(nc.semaphore(name))

        ident, pair_sum = sb("ident2", [P, P]), sb("pair_sum", [P, P])
        gain = sb("gain", [P, 1])
        gain8 = sb("gain8", [P, 1])
        neg_half, eps = sb("neg_half2", [P, 1]), sb("eps2", [P, 1])
        c1_raw, c2_raw = sb("c1_raw", [P, MT, P]), sb("c2_raw", [P, INTER])
        c1_hi, c1_lo = sb("c1_hi", [P, MT, P], f32r), sb("c1_lo", [P, MT, P], f32r)
        c2_split = sb("c2_split", [P, INTER], f32r)
        rank_raw, rank = sb("rank_raw", [P, CHUNK]), sb("rank", [P, CHUNK], bf16)
        attn = [sb(f"attn{i}", [P, N]) for i in range(2)]
        x_in = [sb(f"xr{i}", [P, N]) for i in range(2)]
        x2 = [sb(f"x2{i}", [P, N]) for i in range(2)]
        xT_hi = [sb(f"xT_hi{i}", [P, MT, P], f32r) for i in range(2)]
        xT_lo = [sb(f"xT_lo{i}", [P, MT, P], f32r) for i in range(2)]
        z_split = [sb(f"z_split{i}", [P, P], f32r) for i in range(2)]
        result = [sb(f"result{i}", [P, N]) for i in range(2)]
        sq, norm, inv, xn = sb("sq", [P, N]), sb("norm", [P, N]), sb("inv", [P, N]), sb("xn2", [P, N])
        stats, moments = sb("stats2", [P, 6]), sb("moments2", [P, 2])
        var_eps, rstd = sb("var_eps2", [P, 1]), sb("rstd2", [P, 1])
        NB = CHUNK // SPARSE
        top = [sb(f"top{i}", [P, NB]) for i in range(2)]
        mask = [sb(f"mask{i}", [P, CHUNK], bf16) for i in range(2)]
        ranked = [sb(f"ranked{i}", [P, CHUNK], bf16) for i in range(2)]
        first = [sb(f"first{i}", [P, NB], bf16) for i in range(2)]
        behind = [sb(f"behind{i}", [P, CHUNK], bf16) for i in range(2)]
        h_sb = [sb(f"h_sb{i}", [P, CHUNK]) for i in range(2)]
        hT_hi = [sb(f"hT_hi{i}", [P, CHUNK], f32r) for i in range(2)]
        hT_lo = [sb(f"hT_lo{i}", [P, CHUNK], f32r) for i in range(2)]

        inter = [ps(f"inter{i}", [P, 512]) for i in range(2)]
        hidden = [ps(f"hidden{i}", [P, 512]) for i in range(2)]
        turned = [ps(f"turned{i}", [P, 512]) for i in range(2)]
        acc, pre = ps("acc2", [P, 512]), ps("pre", [P, 512])

        consts_in, consts_done, c_hi, const_step = sem("consts_in2"), sem("consts_done"), sem("c_hi2"), sem("const_step")
        loaded = [sem(f"loaded{i}") for i in range(2)]
        stored = [sem(f"stored2{i}") for i in range(2)]
        squared, norm_mm, norm_root, norm_max, norm_inv = (sem(s) for s in ("squared", "norm_mm", "norm_root", "norm_max", "norm_inv"))
        scaled, added, x_moments, x_var, x_rstd = (sem(s) for s in ("scaled", "added", "x_moments2", "x_var2", "x_rstd2"))
        x_normed, x_turned, xT_hi_done, xT_lo_done = (sem(s) for s in ("x_normed2", "x_turned", "xT_hi_done", "xT_lo_done"))
        z_mm, z_hi, z_lo = sem("z_mm"), sem("z_hi"), sem("z_lo")
        i_mm, i_top, i_mask, i_ranked, i_first, i_sel = (sem(s) for s in ("i_mm", "i_top", "i_mask", "i_ranked", "i_first", "i_sel"))
        h_mm, h_done, h_turned, hT_hi_done, hT_lo_done = (sem(s) for s in ("h_mm", "h_done", "h_turned", "hT_hi_done", "hT_lo_done"))
        o_mm, o_done = sem("o_mm"), sem("o_done")
        powers_set = sem("powers_set2")

        w1 = lambda w, m, off, width: w[:, m * INTER + off:m * INTER + off + width]
        w2 = lambda w, k: w[:, MT * INTER + k * N:MT * INTER + (k + 1) * N]
        blocks = lambda ap: ap.rearrange("p (b s) -> p b s", s=SPARSE)
        spread = lambda ap, nb: ap.unsqueeze(2).broadcast_to([P, nb, SPARSE])
        CONSTS = 6

        def tiles(eng, tile):
            for p in range(3):
                tile(p, p // 2, p % 2, False)
            with eng.Fori(1, TILES // 2 - 1) as k:
                tile(2 * k + 1, k, 1, False)
                tile(2 * k + 2, k + 1, 0, False)
            tile(TILES - 1, TILES // 2 - 1, 1, True)

        with nc.Block() as block:

            @block.sync
            def _(sp):
                def load(p, par):
                    sp.dma_start(attn[par][:], scratch.rearrange("(t b) c n -> t (b c) n", b=2)[p]).then_inc(loaded[par], 16)
                    sp.dma_start(x_in[par][:], A["x"].rearrange("(t b) c n -> t (b c) n", b=2)[p]).then_inc(loaded[par], 16)

                load(0, 0)
                for dst, src in ((pair_sum, "pair_sum"), (gain, "gain"), (ident, "ident"), (c1_raw, "c1T"), (c2_raw, "c2T"), (rank_raw, "rank")):
                    sp.dma_start(dst[:], A[src]).then_inc(consts_in, 16)
                load(1, 1)
                outs = out.rearrange("(t b) c n -> t (b c) n", b=2)

                def body(p, k, par, more):
                    if more:
                        sp.wait_ge(added, p + 1)
                        load(p + 2, par)
                    sp.wait_ge(o_done, p + 1)
                    sp.dma_start(outs[p], result[par][:]).then_inc(stored[par], 16)

                with sp.Fori(0, TILES // 2 - 1) as k:
                    body(2 * k, k, 0, True)
                    body(2 * k + 1, k, 1, True)
                body(TILES - 2, TILES // 2 - 1, 0, False)
                body(TILES - 1, TILES // 2 - 1, 1, False)
                for s in stored:
                    sp.wait_ge(s, 16 * (TILES // 2))

            @block.gpsimd
            def _(pool):
                nc.gpsimd.memset(neg_half[:], -0.5).then_inc(powers_set, 1)
                nc.gpsimd.memset(eps[:], EPS).then_inc(powers_set, 1)
                pool.wait_ge(powers_set, 2)
                pool.wait_ge(consts_done, 1)

                def prepare(a):
                    pool.wait_ge(x_moments, a + 1)
                    nc.gpsimd.tensor_tensor(var_eps[:], moments[:, 1:2], eps[:], ALU.add).then_inc(x_var, 1)
                    pool.wait_ge(x_var, a + 1)
                    nc.gpsimd.tensor_tensor(rstd[:], var_eps[:], neg_half[:], ALU.pow).then_inc(x_rstd, 1)

                def tile(p, k, par, last):
                    def rank_mask(c):
                        use, w = NC * p + c, CHUNKS[c][1]
                        pool.wait_ge(i_mask, use + 1)
                        if later(use - 1):
                            pool.wait_ge(i_sel, use - 1)
                        nc.gpsimd.tensor_tensor(ranked[c % 2][:, 0:w], mask[c % 2][:, 0:w], rank[:, 0:w],
                                                ALU.mult).then_inc(i_ranked, 1)

                    def select(c):
                        use, w = NC * p + c, CHUNKS[c][1]
                        pool.wait_ge(i_first, use + 1)
                        if later(use - 1):
                            pool.wait_ge(h_done, use - 1)
                        nc.gpsimd.tensor_tensor(blocks(behind[c % 2][:, 0:w]), blocks(ranked[c % 2][:, 0:w]),
                                                spread(first[c % 2][:, 0:w // SPARSE], w // SPARSE),
                                                ALU.subtract).then_inc(i_sel, 1)

                    rank_mask(0)
                    rank_mask(1)
                    select(0)
                    select(1)
                    rank_mask(2)
                    if not last:
                        prepare(p + 1)
                    select(2)
                    rank_mask(3)
                    select(3)

                prepare(0)
                tiles(pool, tile)

            @block.scalar
            def _(act):
                def square(a, pair, par):
                    act.wait_ge(loaded[par], 32 * (pair + 1))
                    if later(a):
                        act.wait_ge(norm_mm, a)
                    nc.scalar.activation(sq[:], attn[par][:], ACT.Square).then_inc(squared, 1)

                def root(a):
                    act.wait_ge(norm_mm, a + 1)
                    if later(a):
                        act.wait_ge(scaled, a)
                    nc.scalar.activation(norm[:], pre[:], ACT.Sqrt).then_inc(norm_root, 1)

                def x_high(a, par):
                    act.wait_ge(x_turned, a + 1)
                    if later(NC * (a - 1)):
                        act.wait_ge(h_mm, NC * (a - 1))
                    nc.scalar.activation(xT_hi[par][:], pre[:].rearrange("p (m n) -> p m n", m=MT),
                                         ACT.Copy).then_inc(xT_hi_done, 1)

                def z_high(a, par):
                    act.wait_ge(z_mm, a + 1)
                    if later(NC * (a - 1)):
                        act.wait_ge(i_mm, NC * (a - 1))
                    nc.scalar.activation(z_split[par][:], pre[:, 0:P], ACT.Copy).then_inc(z_hi, 1)

                def tile(p, k, par, last):
                    def h_high(c):
                        use, w = NC * p + c, CHUNKS[c][1]
                        act.wait_ge(h_turned, use + 1)
                        if later(use - 1):
                            act.wait_ge(o_mm, use - 1)
                        nc.scalar.activation(hT_hi[c % 2][:, 0:w], turned[c % 2][:, 0:w], ACT.Relu).then_inc(hT_hi_done, 1)

                    if not last:
                        square(p + 1, k if par == 0 else k + 1, 1 - par)
                        root(p + 1)
                    h_high(0)
                    h_high(1)
                    if not last:
                        x_high(p + 1, 1 - par)
                    h_high(2)
                    if not last:
                        z_high(p + 1, 1 - par)
                    h_high(3)

                square(0, 0, 0)
                root(0)
                x_high(0, 0)
                z_high(0, 0)
                tiles(act, tile)

            @block.vector
            def _(dve):
                dve.wait_ge(consts_in, 16 * CONSTS)
                nc.vector.tensor_scalar(gain8[:], gain[:], float(C) ** 0.5, None, ALU.mult).then_inc(const_step, 1)
                nc.vector.tensor_copy(rank[:], rank_raw[:]).then_inc(consts_done, 1)
                nc.vector.tensor_copy(c1_hi[:], c1_raw[:]).then_inc(c_hi, 1)
                nc.vector.tensor_copy(c2_split[:], c2_raw[:]).then_inc(c_hi, 1)
                dve.wait_ge(const_step, 1)
                dve.wait_ge(c_hi, 2)
                nc.vector.tensor_tensor(c1_lo[:], c1_raw[:], c1_hi[:].bitcast(fp32), ALU.subtract).then_inc(consts_done, 1)
                for r in (SPARSE, 3 * SPARSE):
                    q = slice(r, r + SPARSE)
                    nc.vector.tensor_tensor(c2_split[q, :], c2_raw[q, :], c2_split[q, :].bitcast(fp32),
                                            ALU.subtract).then_inc(consts_done, 1)

                def residual(a, par):
                    dve.wait_ge(norm_root, a + 1)
                    nc.vector.tensor_scalar(norm[:], norm[:], NORM_EPS, None, ALU.max).then_inc(norm_max, 1)
                    dve.wait_ge(norm_max, a + 1)
                    nc.vector.reciprocal(inv[:], norm[:]).then_inc(norm_inv, 1)
                    dve.wait_ge(norm_inv, a + 1)
                    nc.vector.scalar_tensor_tensor(inv[:], attn[par][:], gain8[:, 0:1], inv[:], ALU.mult,
                                                   ALU.mult).then_inc(scaled, 1)
                    dve.wait_ge(scaled, a + 1)
                    if later(a - 1):
                        dve.wait_ge(o_done, a - 1)
                    nc.vector.tensor_tensor(x2[par][:], inv[:], x_in[par][:], ALU.add).then_inc(added, 1)
                    dve.wait_ge(added, a + 1)
                    nc.vector.bn_stats(stats[:], x2[par][:])
                    dve.drain()
                    nc.vector.bn_aggr(moments[:], stats[:]).then_inc(x_moments, 1)

                def normalize(a, par):
                    dve.wait_ge(x_rstd, a + 1)
                    if later(a):
                        dve.wait_ge(x_turned, a)
                    nc.vector.tensor_scalar(xn[:], x2[par][:], moments[:, 0:1], rstd[:], ALU.subtract,
                                            ALU.mult).then_inc(x_normed, 1)

                def x_low(a, par):
                    dve.wait_ge(xT_hi_done, a + 1)
                    nc.vector.tensor_tensor(xT_lo[par][:], pre[:].rearrange("p (m n) -> p m n", m=MT),
                                            xT_hi[par][:].bitcast(fp32), ALU.subtract).then_inc(xT_lo_done, 1)

                def z_low(a, par):
                    dve.wait_ge(z_hi, a + 1)
                    nc.vector.tensor_tensor(z_split[par][C:P, :], pre[C:P, 0:P], z_split[par][C:P, :].bitcast(fp32),
                                            ALU.subtract).then_inc(z_lo, 1)

                def tile(p, k, par, last):
                    def block_max(c):
                        use, w = NC * p + c, CHUNKS[c][1]
                        nb = w // SPARSE
                        dve.wait_ge(i_mm, use + 1)
                        nc.vector.tensor_reduce(top[c % 2][:, 0:nb], blocks(inter[c % 2][:, 0:w]), AX.X,
                                                ALU.max).then_inc(i_top, 1)
                        dve.wait_ge(i_top, use + 1)
                        if later(use - 1):
                            dve.wait_ge(i_ranked, use - 1)
                        nc.vector.tensor_tensor(blocks(mask[c % 2][:, 0:w]), blocks(inter[c % 2][:, 0:w]),
                                                spread(top[c % 2][:, 0:nb], nb), ALU.is_ge).then_inc(i_mask, 1)

                    def first_max(c):
                        use, w = NC * p + c, CHUNKS[c][1]
                        dve.wait_ge(i_ranked, use + 1)
                        if later(use - 1):
                            dve.wait_ge(i_sel, use - 1)
                        nc.vector.tensor_reduce(first[c % 2][:, 0:w // SPARSE], blocks(ranked[c % 2][:, 0:w]), AX.X,
                                                ALU.max).then_inc(i_first, 1)

                    def gate(c):
                        use, w = NC * p + c, CHUNKS[c][1]
                        dve.wait_ge(i_sel, use + 1)
                        dve.wait_ge(h_mm, use + 1)
                        if later(use - 1):
                            dve.wait_ge(h_turned, use - 1)
                        nc.vector.scalar_tensor_tensor(h_sb[c % 2][:, 0:w], behind[c % 2][:, 0:w], 0.0,
                                                       hidden[c % 2][:, 0:w], ALU.is_equal, ALU.mult)\
                            .then_inc(h_done, 1)

                    def h_low(c):
                        use, w = NC * p + c, CHUNKS[c][1]
                        dve.wait_ge(hT_hi_done, use + 1)
                        nc.vector.scalar_tensor_tensor(hT_lo[c % 2][:, 0:w], turned[c % 2][:, 0:w], 0.0,
                                                       hT_hi[c % 2][:, 0:w].bitcast(fp32), ALU.max,
                                                       ALU.subtract).then_inc(hT_lo_done, 1)

                    block_max(0)
                    block_max(1)
                    first_max(0)
                    first_max(1)
                    gate(0)
                    if not last:
                        residual(p + 1, 1 - par)
                    gate(1)
                    h_low(0)
                    block_max(2)
                    if not last:
                        normalize(p + 1, 1 - par)
                    first_max(2)
                    gate(2)
                    h_low(1)
                    if not last:
                        x_low(p + 1, 1 - par)
                    block_max(3)
                    first_max(3)
                    gate(3)
                    h_low(2)
                    if not last:
                        z_low(p + 1, 1 - par)
                    h_low(3)
                    dve.wait_ge(o_mm, NC * (p + 1))
                    if later(16 * k):
                        dve.wait_ge(stored[par], 16 * k)
                    nc.vector.tensor_tensor(result[par][:], acc[:], x2[par][:], ALU.add).then_inc(o_done, 1)

                residual(0, 0)
                normalize(0, 0)
                x_low(0, 0)
                z_low(0, 0)
                tiles(dve, tile)

            @block.tensor
            def _(pe):
                pe.wait_ge(consts_in, 16 * CONSTS)
                pe.wait_ge(consts_done, 4)

                def norms(a):
                    pe.wait_ge(squared, a + 1)
                    if later(a):
                        pe.wait_ge(z_lo, a)
                    nc.tensor.matmul(pre[:], pair_sum[:], sq[:], start=True, stop=True).then_inc(norm_mm, 1)

                def turn_x(a, par):
                    pe.wait_ge(x_normed, a + 1)
                    pe.wait_ge(norm_root, a + 1)
                    for m in range(MT):
                        last = nc.tensor.transpose(pre[:, m * P:(m + 1) * P], xn[:, m * P:(m + 1) * P], ident[:])
                    last.then_inc(x_turned, 1)

                def low_rank(a, par):
                    pe.wait_ge(xT_lo_done, a + 1)
                    pairs = [(c1, xT, m) for m in range(MT) for c1 in (c1_hi, c1_lo) for xT in (xT_hi, xT_lo)]
                    for n, (c1, xT, m) in enumerate(pairs):
                        last = nc.tensor.matmul(pre[:, 0:P], c1[:, m, :], xT[par][:, m, :], start=(n == 0),
                                                stop=(n == len(pairs) - 1))
                    last.then_inc(z_mm, 1)

                def tile(p, k, par, last_tile):
                    def project(c):
                        use, (off, w) = NC * p + c, CHUNKS[c]
                        if c == 0:
                            pe.wait_ge(z_lo, p + 1)
                        if later(use - 1):
                            pe.wait_ge(i_mask, use - 1)
                        nc.tensor.matmul(inter[c % 2][:, 0:w], z_split[par][:], c2_split[:, off:off + w],
                                         start=True, stop=True).then_inc(i_mm, 1)

                    def hide(c):
                        use, (off, w) = NC * p + c, CHUNKS[c]
                        if later(use - 1):
                            pe.wait_ge(h_done, use - 1)
                        terms = [(x, w1(wt, m, off, w), m) for m in range(MT)
                                 for x, wt in ((xT_hi, weights_hi), (xT_hi, weights_lo), (xT_lo, weights_hi))]
                        for n, (x, wt, m) in enumerate(terms):
                            last = nc.tensor.matmul(hidden[c % 2][:, 0:w], x[par][:, m, :], wt, start=(n == 0),
                                                    stop=(n == len(terms) - 1))
                        last.then_inc(h_mm, 1)

                    def turn_h(c):
                        use, w = NC * p + c, CHUNKS[c][1]
                        pe.wait_ge(h_done, use + 1)
                        if later(use - 1):
                            pe.wait_ge(hT_lo_done, use - 1)
                        for i in range(w // P):
                            last = nc.tensor.transpose(turned[c % 2][:, i * P:(i + 1) * P],
                                                       h_sb[c % 2][:, i * P:(i + 1) * P], ident[:])
                        last.then_inc(h_turned, 1)

                    def down(c):
                        use, (off, w) = NC * p + c, CHUNKS[c]
                        pe.wait_ge(hT_lo_done, use + 1)
                        if c == 0:
                            if later(p):
                                pe.wait_ge(o_done, p)
                        for i in range(w // P):
                            kt, cols = off // P + i, slice(i * P, (i + 1) * P)
                            for n, (h, wt) in enumerate(((hT_hi, weights_hi), (hT_hi, weights_lo), (hT_lo, weights_hi))):
                                last = nc.tensor.matmul(acc[:], h[c % 2][:, cols], w2(wt, kt),
                                                        start=(kt == 0 and n == 0), stop=(kt == KT - 1 and n == 2))
                        last.then_inc(o_mm, 1)

                    project(0)
                    project(1)
                    hide(0)
                    if not last_tile:
                        norms(p + 1)
                    hide(1)
                    turn_h(0)
                    project(2)
                    hide(2)
                    turn_h(1)
                    down(0)
                    if not last_tile:
                        turn_x(p + 1, 1 - par)
                    project(3)
                    hide(3)
                    turn_h(2)
                    down(1)
                    if not last_tile:
                        low_rank(p + 1, 1 - par)
                    turn_h(3)
                    down(2)
                    down(3)

                norms(0)
                turn_x(0, 0)
                low_rank(0, 0)
                tiles(pe, tile)


def build(nc, A, out):
    scratch = nc.dram_tensor("attn_out", (B, C, N), fp32, kind="Internal").ap()
    with nc.sbuf_tensor("weights_hi", [P, FFN_COLS], f32r) as weights_hi, \
         nc.sbuf_tensor("weights_lo", [P, FFN_COLS], f32r) as weights_lo:
        attention_phase(nc, A, weights_hi, weights_lo, scratch)
        ffn_phase(nc, A, weights_hi, weights_lo, scratch, out)


def kernel(x, ctx_4096, L0_xattn_Wq, L0_xattn_Wk, L0_xattn_Wv, L0_xattn_Wo, L0_xattn_bo, L0_xattn_g,
           L0_ffn_c1_w, L0_ffn_c2_w, L0_ffn_w1, L0_ffn_w2t):
    import numpy as np
    from concourse import bacc
    from concourse.bass_utils import run_bass_kernel_spmd

    x, ctx = np.asarray(x), np.asarray(ctx_4096)
    Wq, Wk, Wv, Wo = (np.asarray(w) for w in (L0_xattn_Wq, L0_xattn_Wk, L0_xattn_Wv, L0_xattn_Wo))
    c1, c2, w1, w2t = (np.asarray(w) for w in (L0_ffn_c1_w, L0_ffn_c2_w, L0_ffn_w1, L0_ffn_w2t))
    g = np.asarray(L0_xattn_g).reshape(C, 1)
    ffn_w = np.concatenate([w1.T.reshape(MT, P, INTER).transpose(1, 0, 2).reshape(P, -1),
                            w2t.reshape(KT, P, N).transpose(1, 0, 2).reshape(P, -1)], axis=1)
    c1_rows = np.zeros((4, SPARSE, N), np.float32)
    c1_rows[:, :RANK] = c1
    c2_rows = np.zeros((4, SPARSE, INTER), np.float32)
    c2_rows[:, :RANK] = c2.T
    arrays = {
        "x": x,
        "ctx": ctx,
        "ctxT": ctx.transpose(0, 2, 1).reshape(B, NT, P, C).transpose(0, 2, 1, 3),
        "wqk": np.stack([np.concatenate([w.T, w.T], axis=0) for w in (Wq, Wk)], axis=1),
        "wv": Wv.reshape(HEADS, D, C).transpose(1, 0, 2),
        "woT": Wo.T.reshape(HEADS, D, C).transpose(1, 0, 2),
        "bo": np.asarray(L0_xattn_bo).reshape(C, 1),
        "gain": np.concatenate([g, g], axis=0),
        "c1T": c1_rows.reshape(P, MT, P).transpose(2, 1, 0),
        "c2T": c2_rows.reshape(P, INTER),
        "ffn_w": ffn_w.reshape(P, B, SPLIT).transpose(1, 0, 2),
        "ident": np.eye(P, dtype=np.float32),
        "pair_sum": np.kron(np.eye(P // C, dtype=np.float32), np.ones((C, C), np.float32)),
        "rank": np.tile(np.arange(SPARSE, 0, -1).astype(np.float32), (P, CHUNK // SPARSE)),
    }
    arrays = {name: np.ascontiguousarray(a) for name, a in arrays.items()}
    nc = bacc.Bacc("TRN2", target_bir_lowering=False, num_devices=1)
    A = {name: nc.dram_tensor("in_" + name, a.shape, mybir.dt.from_np(a.dtype), kind="ExternalInput").ap()
         for name, a in arrays.items()}
    out = nc.dram_tensor("out", (B, C, N), fp32, kind="ExternalOutput").ap()
    build(nc, A, out)
    return run_bass_kernel_spmd(nc, [{"in_" + name: a for name, a in arrays.items()}], core_ids=[0]).results[0]["out"]
```

```python
from contextlib import ExitStack

import concourse.bass as bass
from concourse import mybir

fp32 = mybir.dt.float32
f32r = mybir.dt.float32r
bf16 = mybir.dt.bfloat16
ALU = mybir.AluOpType
ACT = mybir.ActivationFunctionType
AX = mybir.AxisListType

B, C, N = 32, 64, 512
HEADS, D = 8, 64
HID = HEADS * D
P = 128
NT = N // P
HT = HID // P
SCALE = float(D) ** -0.5
EPS = 1e-5
NORM_EPS = 1e-12
INTER, SPARSE, RANK = 1792, 32, 16
MT = N // P
KT = INTER // P
FFN_COLS = MT * INTER + KT * N
SPLIT = FFN_COLS // B
TILES = B * C // P
CHUNK = 512
CHUNKS = [(off, min(CHUNK, INTER - off)) for off in range(0, INTER, CHUNK)]
NC = len(CHUNKS)
FIRST_LOOPED, LAST_LOOPED = 5, B - 4


def later(value):
    return not isinstance(value, int) or value > 0


def steps(eng, step):
    for g in range(-1, FIRST_LOOPED):
        step(g, g // 2, g % 2, g)
    with eng.Fori(FIRST_LOOPED // 2, LAST_LOOPED // 2) as k:
        step(2 * k + 1, k, 1, None)
        step(2 * k + 2, k + 1, 0, None)
    for g in range(LAST_LOOPED + 1, B + 2):
        step(g, g // 2, g % 2, g)


def real(known, shift):
    return known is None or 0 <= known + shift < B


def attention_phase(nc, A, shared, scratch):
    with ExitStack() as ctx:
        sb = lambda name, shape, dt=fp32: ctx.enter_context(nc.sbuf_tensor(name, shape, dt))
        ps = lambda name, shape: ctx.enter_context(nc.psum_tensor(name, shape, fp32))
        sem = lambda name: ctx.enter_context(nc.semaphore(name))

        weights_hi, weights_lo = shared["weights_hi"], shared["weights_lo"]
        wq_hi, wq_lo = sb("wq_hi", [P, HID], f32r), sb("wq_lo", [P, HID], f32r)
        wk_hi, wk_lo = sb("wk_hi", [P, HID], f32r), sb("wk_lo", [P, HID], f32r)
        vo = sb("vo", [C, HEADS, C])
        bo = sb("bo", [P, 1])
        ident = shared["ident"]
        stage = [sb(f"stage{i}", [P, SPLIT]) for i in range(2)]
        x_in = [sb(f"x_in{i}", [P, N]) for i in range(2)]
        c_in = [sb(f"c_in{i}", [P, N]) for i in range(2)]
        ctxT = [sb(f"ctxT{i}", [P, NT, C]) for i in range(2)]
        x_split = [sb(f"x_split{i}", [P, N], f32r) for i in range(2)]
        c_split = [sb(f"c_split{i}", [P, N], f32r) for i in range(2)]
        xn = sb("xn", [P, N])
        stats = sb("stats", [P, 6])
        moments = [sb(f"moments{i}", [P, 2]) for i in range(2)]
        var_eps = sb("var_eps", [P, 1])
        neg_half, eps = shared["neg_half"], shared["eps"]
        rstd = [sb(f"rstd{i}", [P, 1]) for i in range(2)]
        E = [sb(f"E{i}", [P, HT, N]) for i in range(2)]
        neg_kmax = [sb(f"neg_kmax{i}", [P, HT]) for i in range(2)]
        ksum = [sb(f"ksum{i}", [P, HT]) for i in range(2)]
        krec = sb("krec", [P, HT])
        Q = [sb(f"Q{i}", [P, NT, HID]) for i in range(2)]
        HALF = NT * HEADS // 2
        w_raw = E[1][:, 0:2, :]
        wv, woT = (Q[0][0:D, t, :].rearrange("e (h c) -> e h c", h=HEADS) for t in range(2))
        c2_raw = Q[1][:].rearrange("p t n -> p (t n)")[:, 0:INTER]
        qmax = sb("qmax", [P, 2, HALF])
        qsum = sb("qsum", [P, 2, HALF])
        qrec = [sb(f"qrec{i}", [P, 2, HALF]) for i in range(2)]
        ET = [sb(f"ET{i}", [P, HID]) for i in range(2)]
        QT = [sb(f"QT{i}", [P, N]) for i in range(2)]
        PT = sb("PT", [C, HID])
        G = [sb(f"G{i}", [P, HT, C]) for i in range(2)]
        out_sb = [sb(f"out_sb{i}", [P, N]) for i in range(2)]
        c1_raw, rank_raw = out_sb[0][:], out_sb[1][:]

        slot = [ps(f"slot{i}", [P, 2, 512]) for i in range(2)]
        turn_e, turn_q = ps("turn_e", [P, 512]), ps("turn_q", [P, 512])
        pg = ps("pg", [P, 512])
        acc = ps("acc", [P, 512])

        consts_in, ffn_consts_in, ffn_consts_hi = sem("consts_in"), sem("ffn_consts_in"), sem("ffn_consts_hi")
        ffn_consts_done = sem("ffn_consts_done")
        w_hi, w_lo, vo_mm, vo_ready = sem("w_hi"), sem("w_lo"), sem("vo_mm"), sem("vo_ready")
        x_loaded = [sem(f"x_loaded{i}") for i in range(2)]
        c_loaded = [sem(f"c_loaded{i}") for i in range(2)]
        ctxT_loaded = [sem(f"ctxT_loaded{i}") for i in range(2)]
        stage_loaded = [sem(f"stage_loaded{i}") for i in range(2)]
        stage_hi, stage_done = sem("stage_hi"), sem("stage_done")
        x_moments, x_var, x_rstd = sem("x_moments"), sem("x_var"), sem("x_rstd")
        x_normed, x_hi, x_ready = sem("x_normed"), sem("x_hi"), sem("x_ready")
        c_hi, c_ready = sem("c_hi"), sem("c_ready")
        k_proj, k_max, k_exped, k_rec = sem("k_proj"), sem("k_max"), sem("k_exped"), sem("k_rec")
        q_proj, q_max, q_shifted, q_exped = sem("q_proj"), sem("q_max"), sem("q_shifted"), sem("q_exped")
        q_sum, q_rec, q_scaled = sem("q_sum"), sem("q_rec"), sem("q_scaled")
        e_turned, e_copied, p_mm, p_copied = sem("e_turned"), sem("e_copied"), sem("p_mm"), sem("p_copied")
        q_turned, q_copied, out_mm, out_copied = sem("q_turned"), sem("q_copied"), sem("out_mm"), sem("out_copied")
        g_mm, g_ready = sem("g_mm"), sem("g_ready")
        stored = [sem(f"stored{i}") for i in range(2)]
        powers_set = sem("powers_set")

        heads = lambda ap: ap.rearrange("p a (h d) -> p (a h) d", d=D)
        CONSTS, FFN_CONSTS = 5, 5

        with nc.Block() as block:

            @block.sync
            def _(sp):
                def load_x(g, k, par):
                    for r in (0, C):
                        sp.dma_start(x_in[par][r:r + C, :], A["x"][g]).then_inc(x_loaded[par], 16)

                def load_c(g, k, par):
                    for r in (0, C):
                        sp.dma_start(c_in[par][r:r + C, :], A["ctx"][g]).then_inc(c_loaded[par], 16)

                def load_ctxT(g, par):
                    sp.dma_start(ctxT[par][:], A["ctxT"][g]).then_inc(ctxT_loaded[par], 16)

                def load_stage(g, par):
                    sp.dma_start(stage[par][:], A["ffn_w"][g]).then_inc(stage_loaded[par], 16)

                load_x(0, 0, 0)
                sp.dma_start(w_raw, A["wqk"]).then_inc(consts_in, 16)
                load_c(0, 0, 0)
                sp.dma_start(wv, A["wv"]).then_inc(consts_in, 16)
                sp.dma_start(woT, A["woT"]).then_inc(consts_in, 16)
                sp.dma_start(bo[C:P, :], A["bo"]).then_inc(consts_in, 16)
                sp.dma_start(ident[:], A["ident"]).then_inc(consts_in, 16)
                load_x(1, 0, 1)
                load_c(1, 0, 1)
                load_ctxT(0, 0)
                load_stage(0, 0)
                load_stage(1, 1)
                for dst, src in ((c1_raw, "c1T"), (rank_raw, "rank"), (shared["gain8"][:], "gain"),
                                 (shared["batch_of"][:], "batch_of"), (c2_raw, "c2T")):
                    sp.dma_start(dst, A[src]).then_inc(ffn_consts_in, 16)

                def step(g, k, par, known):
                    if known == -1:
                        return
                    if real(known, 2):
                        sp.wait_ge(x_ready, g + 1)
                        load_x(g + 2, k + 1, par)
                        sp.wait_ge(c_ready, g + 1)
                        load_c(g + 2, k + 1, par)
                        sp.wait_ge(stage_done, g + 1)
                        load_stage(g + 2, par)
                    if real(known, 1):
                        if later(NT * g):
                            sp.wait_ge(p_mm, NT * g)
                        load_ctxT(g + 1, 1 - par)
                    if real(known, -2):
                        sp.wait_ge(out_copied, g - 1)
                        sp.dma_start(scratch[g - 2], out_sb[par][C:P, :]).then_inc(stored[par], 16)

                steps(sp, step)
                for s in stored:
                    sp.wait_ge(s, 16 * (B // 2))

            @block.gpsimd
            def _(pool):
                nc.gpsimd.memset(neg_half[:], -0.5).then_inc(powers_set, 1)
                nc.gpsimd.memset(eps[:], EPS).then_inc(powers_set, 1)
                pool.wait_ge(powers_set, 2)

                def step(g, k, par, known):
                    if later(g + 1 if known is None else min(g + 1, B)):
                        pool.wait_ge(c_ready, g + 1 if known is None else min(g + 1, B))
                    if real(known, 0):
                        cols = bass.ds(g * SPLIT, SPLIT)
                        pool.wait_ge(stage_loaded[par], 16 * (k + 1))
                        nc.gpsimd.tensor_copy(weights_hi[:, cols], stage[par][:]).then_inc(stage_hi, 1)
                        pool.wait_ge(stage_hi, g + 1)
                        nc.gpsimd.tensor_tensor(weights_lo[:, cols], stage[par][:],
                                                weights_hi[:, cols].bitcast(fp32),
                                                ALU.subtract).then_inc(stage_done, 1)
                    if real(known, 1):
                        pool.wait_ge(x_moments, g + 2)
                        nc.gpsimd.tensor_tensor(var_eps[:], moments[1 - par][:, 1:2], eps[:],
                                                ALU.add).then_inc(x_var, 1)
                        pool.wait_ge(x_var, g + 2)
                        nc.gpsimd.tensor_tensor(rstd[1 - par][:], var_eps[:], neg_half[:],
                                                ALU.pow).then_inc(x_rstd, 1)
                    if real(known, -1):
                        for s in range(2):
                            pool.wait_ge(q_rec, 2 * g - 1 + s)
                            half = heads(Q[1 - par][:, 2 * s:2 * s + 2, :])
                            nc.gpsimd.tensor_tensor(
                                half, half, qrec[1 - par][:, s, :].unsqueeze(2).broadcast_to([P, HALF, D]),
                                ALU.mult).then_inc(q_scaled, 1)
                    if real(known, 1):
                        pool.wait_ge(x_rstd, g + 2)
                        if later(g + 1):
                            pool.wait_ge(stage_done, g + 1)
                        if later(2 * g):
                            pool.wait_ge(q_scaled, 2 * g)
                        pool.wait_ge(x_hi, g + 2)
                        nc.gpsimd.tensor_tensor(x_split[1 - par][C:P, :], xn[C:P, :],
                                                x_split[1 - par][C:P, :].bitcast(fp32),
                                                ALU.subtract).then_inc(x_ready, 1)
                        pool.wait_ge(c_hi, g + 2)
                        nc.gpsimd.tensor_tensor(c_split[1 - par][C:P, :], c_in[1 - par][C:P, :],
                                                c_split[1 - par][C:P, :].bitcast(fp32),
                                                ALU.subtract).then_inc(c_ready, 1)

                steps(pool, step)

            @block.vector
            def _(dve):
                def prologue():
                    dve.wait_ge(consts_in, 16 * CONSTS)
                    for n, (hi, lo) in enumerate(((wq_hi, wq_lo), (wk_hi, wk_lo))):
                        nc.vector.tensor_copy(hi[:], w_raw[:, n, :]).then_inc(w_hi, 1)
                        dve.wait_ge(w_hi, n + 1)
                        nc.vector.tensor_tensor(lo[:], w_raw[:, n, :], hi[:].bitcast(fp32),
                                                ALU.subtract).then_inc(w_lo, 1)
                    dve.wait_ge(vo_mm, 1)
                    nc.vector.tensor_copy(vo[:], acc[0:C, :].rearrange("c (h o) -> c h o", h=HEADS))\
                        .then_inc(vo_ready, 1)

                def split_ffn_constants():
                    c1_hi, c1_lo, c2_split = (shared[n] for n in ("c1_hi", "c1_lo", "c2_split"))
                    dve.wait_ge(ffn_consts_in, 16 * FFN_CONSTS)
                    nc.vector.tensor_copy(c1_hi[:], c1_raw).then_inc(ffn_consts_hi, 1)
                    nc.vector.tensor_copy(c2_split[:], c2_raw).then_inc(ffn_consts_hi, 1)
                    nc.vector.tensor_copy(shared["rank"][:], rank_raw).then_inc(ffn_consts_done, 1)
                    nc.vector.tensor_scalar(shared["gain8"][:], shared["gain8"][:], float(C) ** 0.5, None,
                                            ALU.mult).then_inc(ffn_consts_done, 1)
                    dve.wait_ge(ffn_consts_hi, 2)
                    nc.vector.tensor_tensor(c1_lo[:], c1_raw, c1_hi[:].bitcast(fp32), ALU.subtract)\
                        .then_inc(ffn_consts_done, 1)
                    for r in (SPARSE, 3 * SPARSE):
                        q = slice(r, r + SPARSE)
                        nc.vector.tensor_tensor(c2_split[q, :], c2_raw[q, :], c2_split[q, :].bitcast(fp32),
                                                ALU.subtract).then_inc(ffn_consts_done, 1)

                def step(g, k, par, known):
                    def gains():
                        if real(known, -2):
                            dve.wait_ge(k_rec, g - 1)
                            dve.wait_ge(g_mm, g - 1)
                            nc.vector.scalar_tensor_tensor(
                                G[par][:], pg[:, 0:HT * C].rearrange("p (j o) -> p j o", j=HT), SCALE,
                                krec[:].unsqueeze(2).broadcast_to([P, HT, C]), ALU.mult, ALU.mult)\
                                .then_inc(g_ready, 1)

                    if real(known, -1):
                        for s in range(2):
                            dve.wait_ge(q_proj, 2 * g - 1 + s)
                            src = heads(slot[s][:])
                            nc.vector.tensor_reduce(qmax[:, s, :], src, AX.X, ALU.max).then_inc(q_max, 1)
                            dve.wait_ge(q_max, 2 * g - 1 + s)
                            if known == 2:
                                dve.wait_ge(ffn_consts_done, 5)
                            if later(HT * (g - 2)):
                                dve.wait_ge(q_turned, HT * (g - 2))
                            nc.vector.tensor_tensor(
                                heads(Q[1 - par][:, 2 * s:2 * s + 2, :]), src,
                                qmax[:, s, :].unsqueeze(2).broadcast_to([P, HALF, D]),
                                ALU.subtract).then_inc(q_shifted, 1)
                            if s == 0:
                                gains()
                    else:
                        gains()
                    if known == -1:
                        prologue()
                    if real(known, 0):
                        for s in range(2):
                            dve.wait_ge(k_proj, 2 * g + s + 1)
                            nc.vector.tensor_reduce(neg_kmax[par][:, 2 * s:2 * s + 2], slot[s][:], AX.X, ALU.max,
                                                    negate=True).then_inc(k_max, 1)
                    if real(known, 1):
                        dve.wait_ge(x_loaded[1 - par], 32 * ((k if par == 0 else k + 1) + 1))
                        nc.vector.bn_stats(stats[:], x_in[1 - par][:])
                        dve.drain()
                        nc.vector.bn_aggr(moments[1 - par][:], stats[:]).then_inc(x_moments, 1)
                    if real(known, -1):
                        for s in range(2):
                            dve.wait_ge(q_exped, 2 * g - 1 + s)
                            nc.vector.tensor_reduce(qsum[:, s, :], heads(Q[1 - par][:, 2 * s:2 * s + 2, :]),
                                                    AX.X, ALU.add).then_inc(q_sum, 1)
                            dve.wait_ge(q_sum, 2 * g - 1 + s)
                            if later(2 * g - 4):
                                dve.wait_ge(q_scaled, 2 * g - 4)
                            nc.vector.reciprocal(qrec[1 - par][:, s, :], qsum[:, s, :]).then_inc(q_rec, 1)
                    if real(known, -1):
                        dve.wait_ge(k_exped, 2 * g)
                        nc.vector.reciprocal(krec[:], ksum[1 - par][:]).then_inc(k_rec, 1)
                    if real(known, 1):
                        dve.wait_ge(x_rstd, g + 2)
                        if later(g + 1):
                            dve.wait_ge(x_ready, g + 1)
                        nc.vector.tensor_scalar(xn[:], x_in[1 - par][:], moments[1 - par][:, 0:1],
                                                rstd[1 - par][:], ALU.subtract, ALU.mult).then_inc(x_normed, 1)
                        dve.wait_ge(x_normed, g + 2)
                        if later(2 * g):
                            dve.wait_ge(q_proj, 2 * g)
                        nc.vector.tensor_copy(x_split[1 - par][:], xn[:]).then_inc(x_hi, 1)
                    if known == 1:
                        split_ffn_constants()

                steps(dve, step)

            @block.scalar
            def _(act):
                def step(g, k, par, known):
                    if known == 0:
                        act.wait_ge(consts_in, 16 * CONSTS)

                    def exp_q(s):
                        if real(known, -1):
                            act.wait_ge(q_shifted, 2 * g - 1 + s)
                            half = Q[1 - par][:, 2 * s:2 * s + 2, :]
                            nc.scalar.activation(half, half, ACT.Exp).then_inc(q_exped, 1)

                    def exp_k(s):
                        if real(known, 0):
                            act.wait_ge(k_max, 2 * g + s + 1)
                            if later(NT * (g - 1)):
                                act.wait_ge(e_turned, NT * (g - 1))
                            if later(g - 1):
                                act.wait_ge(k_rec, g - 1)
                            for i in range(2):
                                j = 2 * s + i
                                last = nc.scalar.activation(E[par][:, j, :], slot[s][:, i, :], ACT.Exp,
                                                            bias=neg_kmax[par][:, j:j + 1],
                                                            accum_out=ksum[par][:, j:j + 1])
                            last.then_inc(k_exped, 1)

                    def copy(m):
                        if real(known, -1):
                            use = NT * (g - 1) + m
                            act.wait_ge(e_turned, use + 1)
                            if later(use - 1):
                                act.wait_ge(p_mm, use - 1)
                            nc.scalar.activation(ET[m % 2][:], turn_e[:], ACT.Copy).then_inc(e_copied, 1)
                        if real(known, -2):
                            use = HT * (g - 2) + m
                            act.wait_ge(q_turned, use + 1)
                            if later(use - 1):
                                act.wait_ge(out_mm, use - 1)
                            nc.scalar.activation(QT[m % 2][:], turn_q[:], ACT.Copy).then_inc(q_copied, 1)

                    copy(0)
                    exp_q(0)
                    copy(1)
                    exp_q(1)
                    copy(2)
                    exp_k(0)
                    copy(3)
                    exp_k(1)
                    if real(known, 1):
                        act.wait_ge(c_loaded[1 - par], 32 * ((k if par == 0 else k + 1) + 1))
                        if later(2 * g):
                            act.wait_ge(k_proj, 2 * g)
                        nc.scalar.activation(c_split[1 - par][:], c_in[1 - par][:], ACT.Copy).then_inc(c_hi, 1)
                    if real(known, -1):
                        act.wait_ge(p_mm, NT * g)
                        nc.scalar.activation(PT[:], pg[0:C, :], ACT.Copy).then_inc(p_copied, 1)
                    if real(known, -2):
                        if known == 2:
                            act.wait_ge(ffn_consts_done, 5)
                        act.wait_ge(out_mm, HT * (g - 1))
                        if later(16 * (k - 1)):
                            act.wait_ge(stored[par], 16 * (k - 1))
                        nc.scalar.activation(out_sb[par][C:P, :], acc[C:P, :], ACT.Identity,
                                             bias=bo[C:P, :]).then_inc(out_copied, 1)

                steps(act, step)

            @block.tensor
            def _(pe):
                pe.wait_ge(consts_in, 16 * CONSTS)
                for h in range(HEADS):
                    last = nc.tensor.matmul(acc[0:C, h * C:(h + 1) * C], wv[:, h, :], woT[:, h, :],
                                            start=True, stop=True)
                last.then_inc(vo_mm, 1)

                def step(g, k, par, known):
                    if known == -1:
                        return

                    def turn(m):
                        if real(known, -1):
                            if later(NT * (g - 1) + m):
                                pe.wait_ge(e_copied, NT * (g - 1) + m)
                            pe.wait_ge(k_exped, 2 * g)
                            for j in range(HT):
                                last = nc.tensor.transpose(turn_e[:, j * P:(j + 1) * P],
                                                           E[1 - par][:, j, m * P:(m + 1) * P], ident[:])
                            last.then_inc(e_turned, 1)
                        if real(known, -2):
                            if later(HT * (g - 2) + m):
                                pe.wait_ge(q_copied, HT * (g - 2) + m)
                            pe.wait_ge(q_scaled, 2 * g - 2)
                            for t in range(NT):
                                last = nc.tensor.transpose(turn_q[:, t * P:(t + 1) * P],
                                                           Q[par][:, t, m * P:(m + 1) * P], ident[:])
                            last.then_inc(q_turned, 1)

                    def products(m):
                        if real(known, -1):
                            pe.wait_ge(e_copied, NT * (g - 1) + m + 1)
                            if m == 0:
                                pe.wait_ge(ctxT_loaded[1 - par], 16 * ((k - 1 if par == 0 else k) + 1))
                                if later(g - 1):
                                    pe.wait_ge(g_ready, g - 1)
                        if real(known, -2):
                            pe.wait_ge(q_copied, HT * (g - 2) + m + 1)
                            if m == 0:
                                pe.wait_ge(g_ready, g - 1)
                                if later(g - 2):
                                    pe.wait_ge(out_copied, g - 2)
                        if real(known, -1):
                            nc.tensor.matmul(pg[0:C, :], ctxT[1 - par][:, m, :], ET[m % 2][:],
                                             start=(m == 0), stop=(m == NT - 1)).then_inc(p_mm, 1)
                        if real(known, -2):
                            nc.tensor.matmul(acc[C:P, :], G[par][:, m, :], QT[m % 2][:],
                                             start=(m == 0), stop=(m == HT - 1)).then_inc(out_mm, 1)

                    turn(0)
                    if real(known, -2):
                        pe.wait_ge(vo_ready, 1)
                        pe.wait_ge(p_copied, g - 1)
                        for h in range(HEADS):
                            r = (h % 2) * D
                            last = nc.tensor.matmul(pg[r:r + D, (h // 2) * C:(h // 2 + 1) * C],
                                                    PT[:, h * D:(h + 1) * D], vo[:, h, :], start=True, stop=True)
                        last.then_inc(g_mm, 1)
                    turn(1)
                    products(0)
                    if real(known, 0):
                        pe.wait_ge(c_ready, g + 1)
                        pe.wait_ge(w_lo, 2)
                        for s in range(2):
                            if later(2 * g - 1 + s):
                                pe.wait_ge(q_shifted, 2 * g - 1 + s)
                            for i in range(2):
                                j = slice((2 * s + i) * P, (2 * s + i + 1) * P)
                                nc.tensor.matmul(slot[s][:, i, :], wk_hi[:, j], c_split[par][:], start=True, stop=False)
                                last = nc.tensor.matmul(slot[s][:, i, :], wk_lo[:, j], c_split[par][:], start=False, stop=True)
                            last.then_inc(k_proj, 1)
                    turn(2)
                    products(1)
                    turn(3)
                    products(2)
                    products(3)
                    if real(known, 0):
                        pe.wait_ge(x_ready, g + 1)
                        for s in range(2):
                            pe.wait_ge(k_exped, 2 * g + s + 1)
                            for i in range(2):
                                t = slice((2 * s + i) * P, (2 * s + i + 1) * P)
                                nc.tensor.matmul(slot[s][:, i, :], x_split[par][:, t], wq_hi[:], start=True, stop=False)
                                last = nc.tensor.matmul(slot[s][:, i, :], x_split[par][:, t], wq_lo[:], start=False, stop=True)
                            last.then_inc(q_proj, 1)

                steps(pe, step)


def ffn_phase(nc, A, shared, scratch, out):
    with ExitStack() as ctx:
        sb = lambda name, shape, dt=fp32: ctx.enter_context(nc.sbuf_tensor(name, shape, dt))
        ps = lambda name, shape: ctx.enter_context(nc.psum_tensor(name, shape, fp32))
        sem = lambda name: ctx.enter_context(nc.semaphore(name))

        weights_hi, weights_lo = shared["weights_hi"], shared["weights_lo"]
        ident, batch_of, gain8, rank = (shared[n] for n in ("ident", "batch_of", "gain8", "rank"))
        neg_half, eps = shared["neg_half"], shared["eps"]
        c1_hi, c1_lo = (shared[n][:].rearrange("p (m r) -> p m r", m=MT) for n in ("c1_hi", "c1_lo"))
        c2_split = shared["c2_split"]
        attn = [sb(f"attn{i}", [P, N]) for i in range(2)]
        x_in = [sb(f"xr{i}", [P, N]) for i in range(2)]
        x2 = [sb(f"x2{i}", [P, N]) for i in range(2)]
        xT_hi = [sb(f"xT_hi{i}", [P, MT, P], f32r) for i in range(2)]
        xT_lo = [sb(f"xT_lo{i}", [P, MT, P], f32r) for i in range(2)]
        z_split = [sb(f"z_split{i}", [P, P], f32r) for i in range(2)]
        result = [sb(f"result{i}", [P, N]) for i in range(2)]
        sq, scaled_attn, xn = sb("sq", [P, N]), sb("scaled_attn", [P, N]), sb("xn2", [P, N])
        norm, inv, inv_wide = sb("norm", [P, 2 * NT]), sb("inv", [P, 2 * NT]), sb("inv_wide", [P, 2 * NT, C])
        stats, moments = sb("stats2", [P, 6]), sb("moments2", [P, 2])
        var_eps, rstd = sb("var_eps2", [P, 1]), sb("rstd2", [P, 1])
        NB = CHUNK // SPARSE
        top = [sb(f"top{i}", [P, NB]) for i in range(2)]
        mask = [sb(f"mask{i}", [P, CHUNK], bf16) for i in range(2)]
        ranked = [sb(f"ranked{i}", [P, CHUNK], bf16) for i in range(2)]
        first = [sb(f"first{i}", [P, NB], bf16) for i in range(2)]
        behind = [sb(f"behind{i}", [P, CHUNK], bf16) for i in range(2)]
        h_sb = [sb(f"h_sb{i}", [P, CHUNK]) for i in range(2)]
        hT_hi = [sb(f"hT_hi{i}", [P, CHUNK], f32r) for i in range(2)]
        hT_lo = [sb(f"hT_lo{i}", [P, CHUNK], f32r) for i in range(2)]

        inter = [ps(f"inter{i}", [P, 512]) for i in range(2)]
        hidden = [ps(f"hidden{i}", [P, 512]) for i in range(2)]
        turned = [ps(f"turned{i}", [P, 512]) for i in range(2)]
        acc, pre = ps("acc2", [P, 512]), ps("pre", [P, 512])

        loaded = [sem(f"loaded{i}") for i in range(2)]
        stored = [sem(f"stored2{i}") for i in range(2)]
        squared, norm_mm, norm_root, norm_max, norm_inv = (sem(s) for s in ("squared", "norm_mm", "norm_root", "norm_max", "norm_inv"))
        inv_widened, inv_spread = sem("inv_widened"), sem("inv_spread")
        scaled, added, x_moments, x_var, x_rstd = (sem(s) for s in ("scaled", "added", "x_moments2", "x_var2", "x_rstd2"))
        x_normed, x_turned, xT_hi_done, xT_lo_done = (sem(s) for s in ("x_normed2", "x_turned", "xT_hi_done", "xT_lo_done"))
        z_mm, z_hi, z_lo = sem("z_mm"), sem("z_hi"), sem("z_lo")
        i_mm, i_top, i_mask, i_ranked, i_first, i_sel = (sem(s) for s in ("i_mm", "i_top", "i_mask", "i_ranked", "i_first", "i_sel"))
        h_mm, h_done, h_turned, hT_hi_done, hT_lo_done = (sem(s) for s in ("h_mm", "h_done", "h_turned", "hT_hi_done", "hT_lo_done"))
        o_mm, o_done = sem("o_mm"), sem("o_done")

        w1 = lambda w, m, off, width: w[:, m * INTER + off:m * INTER + off + width]
        w2 = lambda w, k: w[:, MT * INTER + k * N:MT * INTER + (k + 1) * N]
        blocks = lambda ap: ap.rearrange("p (b s) -> p b s", s=SPARSE)
        spread = lambda ap, nb: ap.unsqueeze(2).broadcast_to([P, nb, SPARSE])

        def tiles(eng, tile):
            for p in range(3):
                tile(p, p // 2, p % 2, False)
            with eng.Fori(1, TILES // 2 - 1) as k:
                tile(2 * k + 1, k, 1, False)
                tile(2 * k + 2, k + 1, 0, False)
            tile(TILES - 1, TILES // 2 - 1, 1, True)

        with nc.Block() as block:

            @block.sync
            def _(sp):
                def load(p, par):
                    sp.dma_start(attn[par][:], scratch.rearrange("(t b) c n -> t (b c) n", b=2)[p]).then_inc(loaded[par], 16)
                    sp.dma_start(x_in[par][:], A["x"].rearrange("(t b) c n -> t (b c) n", b=2)[p]).then_inc(loaded[par], 16)

                load(0, 0)
                load(1, 1)
                outs = out.rearrange("(t b) c n -> t (b c) n", b=2)

                def body(p, k, par, more):
                    if more:
                        sp.wait_ge(added, p + 1)
                        load(p + 2, par)
                    sp.wait_ge(o_done, p + 1)
                    sp.dma_start(outs[p], result[par][:]).then_inc(stored[par], 16)

                with sp.Fori(0, TILES // 2 - 1) as k:
                    body(2 * k, k, 0, True)
                    body(2 * k + 1, k, 1, True)
                body(TILES - 2, TILES // 2 - 1, 0, False)
                body(TILES - 1, TILES // 2 - 1, 1, False)
                for s in stored:
                    sp.wait_ge(s, 16 * (TILES // 2))

            @block.gpsimd
            def _(pool):
                def prepare(a):
                    pool.wait_ge(x_moments, a + 1)
                    nc.gpsimd.tensor_tensor(var_eps[:], moments[:, 1:2], eps[:], ALU.add).then_inc(x_var, 1)
                    pool.wait_ge(x_var, a + 1)
                    nc.gpsimd.tensor_tensor(rstd[:], var_eps[:], neg_half[:], ALU.pow).then_inc(x_rstd, 1)

                def rank_mask(p, c):
                    use, w = NC * p + c, CHUNKS[c][1]
                    pool.wait_ge(i_mask, use + 1)
                    if later(use - 1):
                        pool.wait_ge(i_sel, use - 1)
                    nc.gpsimd.tensor_tensor(ranked[c % 2][:, 0:w], mask[c % 2][:, 0:w], rank[:, 0:w],
                                            ALU.mult).then_inc(i_ranked, 1)

                def tile(p, k, par, last):
                    def select(c):
                        use, w = NC * p + c, CHUNKS[c][1]
                        pool.wait_ge(i_first, use + 1)
                        if later(use - 1):
                            pool.wait_ge(h_done, use - 1)
                        nc.gpsimd.tensor_tensor(blocks(behind[c % 2][:, 0:w]), blocks(ranked[c % 2][:, 0:w]),
                                                spread(first[c % 2][:, 0:w // SPARSE], w // SPARSE),
                                                ALU.subtract).then_inc(i_sel, 1)

                    select(0)
                    select(1)
                    if not last:
                        prepare(p + 1)
                    rank_mask(p, 2)
                    select(2)
                    rank_mask(p, 3)
                    select(3)
                    if not last:
                        rank_mask(p + 1, 0)
                        rank_mask(p + 1, 1)

                prepare(0)
                rank_mask(0, 0)
                rank_mask(0, 1)
                tiles(pool, tile)

            @block.scalar
            def _(act):
                def square(a, pair, par):
                    act.wait_ge(loaded[par], 32 * (pair + 1))
                    if later(a):
                        act.wait_ge(norm_mm, a)
                    nc.scalar.activation(sq[:], attn[par][:], ACT.Square).then_inc(squared, 1)

                def root(a):
                    act.wait_ge(norm_mm, a + 1)
                    if later(a):
                        act.wait_ge(scaled, a)
                    nc.scalar.activation(norm[:], pre[:, 0:2 * NT], ACT.Sqrt).then_inc(norm_root, 1)

                def x_high(a, par):
                    act.wait_ge(x_turned, a + 1)
                    if later(NC * (a - 1)):
                        act.wait_ge(h_mm, NC * (a - 1))
                    nc.scalar.activation(xT_hi[par][:], pre[:].rearrange("p (m n) -> p m n", m=MT),
                                         ACT.Copy).then_inc(xT_hi_done, 1)

                def z_high(a, par):
                    act.wait_ge(z_mm, a + 1)
                    if later(NC * (a - 1)):
                        act.wait_ge(i_mm, NC * (a - 1))
                    nc.scalar.activation(z_split[par][:], pre[:, 0:P], ACT.Copy).then_inc(z_hi, 1)

                def tile(p, k, par, last):
                    def h_high(c):
                        use, w = NC * p + c, CHUNKS[c][1]
                        act.wait_ge(h_turned, use + 1)
                        if later(use - 1):
                            act.wait_ge(o_mm, use - 1)
                        nc.scalar.activation(hT_hi[c % 2][:, 0:w], turned[c % 2][:, 0:w], ACT.Relu).then_inc(hT_hi_done, 1)

                    if not last:
                        square(p + 1, k if par == 0 else k + 1, 1 - par)
                        root(p + 1)
                    h_high(0)
                    h_high(1)
                    if not last:
                        x_high(p + 1, 1 - par)
                    h_high(2)
                    if not last:
                        z_high(p + 1, 1 - par)
                    h_high(3)

                square(0, 0, 0)
                root(0)
                x_high(0, 0)
                z_high(0, 0)
                tiles(act, tile)

            @block.vector
            def _(dve):
                def inverse_norms(a):
                    dve.wait_ge(norm_root, a + 1)
                    nc.vector.tensor_scalar(norm[:], norm[:], NORM_EPS, None, ALU.max).then_inc(norm_max, 1)
                    dve.wait_ge(norm_max, a + 1)
                    nc.vector.reciprocal(inv[:], norm[:]).then_inc(norm_inv, 1)
                    dve.wait_ge(norm_inv, a + 1)
                    if later(a):
                        dve.wait_ge(inv_spread, a)
                    nc.vector.tensor_copy(inv_wide[:], inv[:].unsqueeze(2).broadcast_to([P, 2 * NT, C]))\
                        .then_inc(inv_widened, 1)

                def residual(a, par):
                    dve.wait_ge(inv_spread, a + 1)
                    nc.vector.scalar_tensor_tensor(scaled_attn[:], attn[par][:], gain8[:, 0:1], pre[:], ALU.mult,
                                                   ALU.mult).then_inc(scaled, 1)
                    dve.wait_ge(scaled, a + 1)
                    if later(a - 1):
                        dve.wait_ge(o_done, a - 1)
                    nc.vector.tensor_tensor(x2[par][:], scaled_attn[:], x_in[par][:], ALU.add).then_inc(added, 1)
                    dve.wait_ge(added, a + 1)
                    nc.vector.bn_stats(stats[:], x2[par][:])
                    dve.drain()
                    nc.vector.bn_aggr(moments[:], stats[:]).then_inc(x_moments, 1)

                def normalize(a, par):
                    dve.wait_ge(x_rstd, a + 1)
                    if later(a):
                        dve.wait_ge(x_turned, a)
                    nc.vector.tensor_scalar(xn[:], x2[par][:], moments[:, 0:1], rstd[:], ALU.subtract,
                                            ALU.mult).then_inc(x_normed, 1)

                def x_low(a, par):
                    dve.wait_ge(xT_hi_done, a + 1)
                    nc.vector.tensor_tensor(xT_lo[par][:], pre[:].rearrange("p (m n) -> p m n", m=MT),
                                            xT_hi[par][:].bitcast(fp32), ALU.subtract).then_inc(xT_lo_done, 1)

                def z_low(a, par):
                    dve.wait_ge(z_hi, a + 1)
                    nc.vector.tensor_tensor(z_split[par][C:P, :], pre[C:P, 0:P], z_split[par][C:P, :].bitcast(fp32),
                                            ALU.subtract).then_inc(z_lo, 1)

                def block_max(p, c):
                    use, w = NC * p + c, CHUNKS[c][1]
                    nb = w // SPARSE
                    dve.wait_ge(i_mm, use + 1)
                    nc.vector.tensor_reduce(top[c % 2][:, 0:nb], blocks(inter[c % 2][:, 0:w]), AX.X,
                                            ALU.max).then_inc(i_top, 1)
                    dve.wait_ge(i_top, use + 1)
                    if later(use - 1):
                        dve.wait_ge(i_ranked, use - 1)
                    nc.vector.tensor_tensor(blocks(mask[c % 2][:, 0:w]), blocks(inter[c % 2][:, 0:w]),
                                            spread(top[c % 2][:, 0:nb], nb), ALU.is_ge).then_inc(i_mask, 1)

                def tile(p, k, par, last):
                    def first_max(c):
                        use, w = NC * p + c, CHUNKS[c][1]
                        dve.wait_ge(i_ranked, use + 1)
                        if later(use - 1):
                            dve.wait_ge(i_sel, use - 1)
                        nc.vector.tensor_reduce(first[c % 2][:, 0:w // SPARSE], blocks(ranked[c % 2][:, 0:w]), AX.X,
                                                ALU.max).then_inc(i_first, 1)

                    def gate(c):
                        use, w = NC * p + c, CHUNKS[c][1]
                        dve.wait_ge(i_sel, use + 1)
                        dve.wait_ge(h_mm, use + 1)
                        if later(use - 1):
                            dve.wait_ge(h_turned, use - 1)
                        nc.vector.scalar_tensor_tensor(h_sb[c % 2][:, 0:w], behind[c % 2][:, 0:w], 0.0,
                                                       hidden[c % 2][:, 0:w], ALU.is_equal, ALU.mult)\
                            .then_inc(h_done, 1)

                    def h_low(c):
                        use, w = NC * p + c, CHUNKS[c][1]
                        dve.wait_ge(hT_hi_done, use + 1)
                        nc.vector.scalar_tensor_tensor(hT_lo[c % 2][:, 0:w], turned[c % 2][:, 0:w], 0.0,
                                                       hT_hi[c % 2][:, 0:w].bitcast(fp32), ALU.max,
                                                       ALU.subtract).then_inc(hT_lo_done, 1)

                    first_max(0)
                    first_max(1)
                    gate(0)
                    if not last:
                        inverse_norms(p + 1)
                    gate(1)
                    h_low(0)
                    if not last:
                        residual(p + 1, 1 - par)
                    block_max(p, 2)
                    if not last:
                        normalize(p + 1, 1 - par)
                    first_max(2)
                    gate(2)
                    h_low(1)
                    if not last:
                        x_low(p + 1, 1 - par)
                    block_max(p, 3)
                    first_max(3)
                    gate(3)
                    h_low(2)
                    if not last:
                        z_low(p + 1, 1 - par)
                    h_low(3)
                    if not last:
                        block_max(p + 1, 0)
                        block_max(p + 1, 1)
                    dve.wait_ge(o_mm, NC * (p + 1))
                    if later(16 * k):
                        dve.wait_ge(stored[par], 16 * k)
                    nc.vector.tensor_tensor(result[par][:], acc[:], x2[par][:], ALU.add).then_inc(o_done, 1)

                inverse_norms(0)
                residual(0, 0)
                normalize(0, 0)
                x_low(0, 0)
                z_low(0, 0)
                block_max(0, 0)
                block_max(0, 1)
                tiles(dve, tile)

            @block.tensor
            def _(pe):
                def norms(a):
                    pe.wait_ge(squared, a + 1)
                    if later(a):
                        pe.wait_ge(z_lo, a)
                    for t in range(NT):
                        last = nc.tensor.matmul(pre[:, 2 * t:2 * t + 2], sq[:, t * P:(t + 1) * P], batch_of[:],
                                                start=True, stop=True)
                    last.then_inc(norm_mm, 1)

                def spread_norms(a):
                    pe.wait_ge(inv_widened, a + 1)
                    for t in range(NT):
                        last = nc.tensor.transpose(pre[:, t * P:(t + 1) * P],
                                                   inv_wide[:, 2 * t:2 * t + 2, :].rearrange("p b c -> p (b c)"),
                                                   ident[:])
                    last.then_inc(inv_spread, 1)

                def turn_x(a, par):
                    pe.wait_ge(x_normed, a + 1)
                    pe.wait_ge(scaled, a + 1)
                    for m in range(MT):
                        last = nc.tensor.transpose(pre[:, m * P:(m + 1) * P], xn[:, m * P:(m + 1) * P], ident[:])
                    last.then_inc(x_turned, 1)

                def low_rank(a, par):
                    pe.wait_ge(xT_lo_done, a + 1)
                    pairs = [(c1, xT, m) for m in range(MT) for c1 in (c1_hi, c1_lo) for xT in (xT_hi, xT_lo)
                             if not (c1 is c1_lo and xT is xT_lo)]
                    for n, (c1, xT, m) in enumerate(pairs):
                        last = nc.tensor.matmul(pre[:, 0:P], c1[:, m, :], xT[par][:, m, :], start=(n == 0),
                                                stop=(n == len(pairs) - 1))
                    last.then_inc(z_mm, 1)

                def project(p, par, c):
                    use, (off, w) = NC * p + c, CHUNKS[c]
                    if c == 0:
                        pe.wait_ge(z_lo, p + 1)
                    if later(use - 1):
                        pe.wait_ge(i_mask, use - 1)
                    nc.tensor.matmul(inter[c % 2][:, 0:w], z_split[par][:], c2_split[:, off:off + w],
                                     start=True, stop=True).then_inc(i_mm, 1)

                def tile(p, k, par, last_tile):
                    def hide(c):
                        use, (off, w) = NC * p + c, CHUNKS[c]
                        if later(use - 1):
                            pe.wait_ge(h_done, use - 1)
                        terms = [(x, w1(wt, m, off, w), m) for m in range(MT)
                                 for x, wt in ((xT_hi, weights_hi), (xT_hi, weights_lo), (xT_lo, weights_hi))]
                        for n, (x, wt, m) in enumerate(terms):
                            last = nc.tensor.matmul(hidden[c % 2][:, 0:w], x[par][:, m, :], wt, start=(n == 0),
                                                    stop=(n == len(terms) - 1))
                        last.then_inc(h_mm, 1)

                    def turn_h(c):
                        use, w = NC * p + c, CHUNKS[c][1]
                        pe.wait_ge(h_done, use + 1)
                        if later(use - 1):
                            pe.wait_ge(hT_lo_done, use - 1)
                        for i in range(w // P):
                            last = nc.tensor.transpose(turned[c % 2][:, i * P:(i + 1) * P],
                                                       h_sb[c % 2][:, i * P:(i + 1) * P], ident[:])
                        last.then_inc(h_turned, 1)

                    def down(c):
                        use, (off, w) = NC * p + c, CHUNKS[c]
                        pe.wait_ge(hT_lo_done, use + 1)
                        if c == 0:
                            if later(p):
                                pe.wait_ge(o_done, p)
                        for i in range(w // P):
                            kt, cols = off // P + i, slice(i * P, (i + 1) * P)
                            for n, (h, wt) in enumerate(((hT_hi, weights_hi), (hT_hi, weights_lo), (hT_lo, weights_hi))):
                                last = nc.tensor.matmul(acc[:], h[c % 2][:, cols], w2(wt, kt),
                                                        start=(kt == 0 and n == 0), stop=(kt == KT - 1 and n == 2))
                        last.then_inc(o_mm, 1)

                    hide(0)
                    if not last_tile:
                        norms(p + 1)
                    hide(1)
                    turn_h(0)
                    if not last_tile:
                        spread_norms(p + 1)
                    project(p, par, 2)
                    hide(2)
                    turn_h(1)
                    down(0)
                    if not last_tile:
                        turn_x(p + 1, 1 - par)
                    project(p, par, 3)
                    hide(3)
                    turn_h(2)
                    down(1)
                    if not last_tile:
                        low_rank(p + 1, 1 - par)
                    turn_h(3)
                    down(2)
                    if not last_tile:
                        project(p + 1, 1 - par, 0)
                        project(p + 1, 1 - par, 1)
                    down(3)

                norms(0)
                spread_norms(0)
                turn_x(0, 0)
                low_rank(0, 0)
                project(0, 0, 0)
                project(0, 0, 1)
                tiles(pe, tile)


def build(nc, A, out):
    scratch = nc.dram_tensor("attn_out", (B, C, N), fp32, kind="Internal").ap()
    with ExitStack() as ctx:
        shared = {name: ctx.enter_context(nc.sbuf_tensor(name, [P, width], dt)) for name, width, dt in (
            ("weights_hi", FFN_COLS, f32r), ("weights_lo", FFN_COLS, f32r), ("c1_hi", MT * P, f32r),
            ("c1_lo", MT * P, f32r), ("c2_split", INTER, f32r), ("rank", CHUNK, bf16), ("ident", P, fp32),
            ("batch_of", 2, fp32), ("gain8", 1, fp32), ("neg_half", 1, fp32), ("eps", 1, fp32))}
        attention_phase(nc, A, shared, scratch)
        ffn_phase(nc, A, shared, scratch, out)


def kernel(x, ctx_4096, L0_xattn_Wq, L0_xattn_Wk, L0_xattn_Wv, L0_xattn_Wo, L0_xattn_bo, L0_xattn_g,
           L0_ffn_c1_w, L0_ffn_c2_w, L0_ffn_w1, L0_ffn_w2t):
    import numpy as np
    from concourse import bacc
    from concourse.bass_utils import run_bass_kernel_spmd

    x, ctx = np.asarray(x), np.asarray(ctx_4096)
    Wq, Wk, Wv, Wo = (np.asarray(w) for w in (L0_xattn_Wq, L0_xattn_Wk, L0_xattn_Wv, L0_xattn_Wo))
    c1, c2, w1, w2t = (np.asarray(w) for w in (L0_ffn_c1_w, L0_ffn_c2_w, L0_ffn_w1, L0_ffn_w2t))
    g = np.asarray(L0_xattn_g).reshape(C, 1)
    ffn_w = np.concatenate([w1.T.reshape(MT, P, INTER).transpose(1, 0, 2).reshape(P, -1),
                            w2t.reshape(KT, P, N).transpose(1, 0, 2).reshape(P, -1)], axis=1)
    c1_rows = np.zeros((4, SPARSE, N), np.float32)
    c1_rows[:, :RANK] = c1
    c2_rows = np.zeros((4, SPARSE, INTER), np.float32)
    c2_rows[:, :RANK] = c2.T
    arrays = {
        "x": x,
        "ctx": ctx,
        "ctxT": ctx.transpose(0, 2, 1).reshape(B, NT, P, C).transpose(0, 2, 1, 3),
        "wqk": np.stack([np.concatenate([w.T, w.T], axis=0) for w in (Wq, Wk)], axis=1),
        "wv": Wv.reshape(HEADS, D, C).transpose(1, 0, 2),
        "woT": Wo.T.reshape(HEADS, D, C).transpose(1, 0, 2),
        "bo": np.asarray(L0_xattn_bo).reshape(C, 1),
        "gain": np.concatenate([g, g], axis=0),
        "c1T": c1_rows.reshape(P, MT, P).transpose(2, 1, 0).reshape(P, MT * P),
        "c2T": c2_rows.reshape(P, INTER),
        "ffn_w": ffn_w.reshape(P, B, SPLIT).transpose(1, 0, 2),
        "ident": np.eye(P, dtype=np.float32),
        "batch_of": np.kron(np.eye(P // C, dtype=np.float32), np.ones((C, 1), np.float32)),
        "rank": np.tile(np.arange(SPARSE, 0, -1).astype(np.float32), (P, CHUNK // SPARSE)),
    }
    arrays = {name: np.ascontiguousarray(a) for name, a in arrays.items()}
    nc = bacc.Bacc("TRN2", target_bir_lowering=False, num_devices=1)
    A = {name: nc.dram_tensor("in_" + name, a.shape, mybir.dt.from_np(a.dtype), kind="ExternalInput").ap()
         for name, a in arrays.items()}
    out = nc.dram_tensor("out", (B, C, N), fp32, kind="ExternalOutput").ap()
    build(nc, A, out)
    return run_bass_kernel_spmd(nc, [{"in_" + name: a for name, a in arrays.items()}], core_ids=[0]).results[0]["out"]
```
